# Optimizing a Trainium2 kernel written in Bass

```python
import numpy as np
import jax
import jax.numpy as jnp

def _softmax(x, axis=-1):
    return jax.nn.softmax(x, axis=axis)

def _gelu(x):
    return jax.nn.gelu(x, approximate=True)

def _silu(x):
    return jax.nn.silu(x)

def _sigmoid(x):
    return jax.nn.sigmoid(x)

def _layernorm(x, axis=-1, eps=1e-05):
    m = jnp.mean(x, axis=axis, keepdims=True)
    v = jnp.var(x, axis=axis, keepdims=True)
    return (x - m) / jnp.sqrt(v + eps)

def _scatter_add(tgt, idx, src, axis=0):
    return tgt.at[idx].add(src)

def _segment_sum(src, seg, n):
    return jax.ops.segment_sum(src, seg, n)
kernel_name = 'mk_adaln_d1_jaxref_r4_ce525b'

def setup_inputs(seed: int=0):
    np.random.seed(seed)
    _w = jnp.asarray

    def _L0_attn_setup():
        import jax, jax.numpy as jnp
        import numpy as np
        D_MODEL = 256
        D_STATE = 16
        D_CONV = 4
        EXPAND = 2
        D_INNER = EXPAND * D_MODEL
        DT_RANK = (D_MODEL + 15) // 16
        BATCH = 2
        SEQ = 512
        EPS = 1e-05

        def _mamba_params(key, scale=0.02):
            ks = jax.random.split(key, 8)
            n = lambda k, s: jax.random.normal(k, s, jnp.float32) * scale
            return {'Win': n(ks[0], (2 * D_INNER, D_MODEL)), 'convw': n(ks[1], (D_INNER, 1, D_CONV)), 'convb': n(ks[2], (D_INNER,)), 'Wx': n(ks[3], (DT_RANK + 2 * D_STATE, D_INNER)), 'Wdt': n(ks[4], (D_INNER, DT_RANK)), 'bdt': n(ks[5], (D_INNER,)), 'Alog': jnp.log(jnp.tile(jnp.arange(1, D_STATE + 1, dtype=jnp.float32), (D_INNER, 1))), 'D': jnp.ones((D_INNER,), jnp.float32), 'Wout': n(ks[6], (D_MODEL, D_INNER))}

        def _mamba(x, Win, convw, convb, Wx, Wdt, bdt, Alog, Dp, Wout):
            B, L, _ = x.shape
            xz = jnp.einsum('bld,ed->ble', x, Win)
            u, z = jnp.split(xz, 2, axis=-1)
            uc = jnp.transpose(u, (0, 2, 1))
            uc = jnp.pad(uc, ((0, 0), (0, 0), (D_CONV - 1, 0)))
            uc = jax.lax.conv_general_dilated(uc, convw, (1,), 'VALID', feature_group_count=D_INNER)
            uc = uc + convb[None, :, None]
            u = jax.nn.silu(jnp.transpose(uc, (0, 2, 1)))
            xdbl = jnp.einsum('bld,ed->ble', u, Wx)
            dtr, Bm, Cm = jnp.split(xdbl, [DT_RANK, DT_RANK + D_STATE], axis=-1)
            dt = jax.nn.softplus(jnp.einsum('blr,dr->bld', dtr, Wdt) + bdt)
            A = -jnp.exp(Alog)

            def step(h, ins):
                dt_t, u_t, B_t, C_t = ins
                h = jnp.exp(dt_t[..., None] * A) * h + (dt_t * u_t)[..., None] * B_t[:, None, :]
                y_t = jnp.einsum('bdn,bn->bd', h, C_t)
                return (h, y_t)
            h0 = jnp.zeros((B, D_INNER, D_STATE), jnp.float32)
            xs = (jnp.moveaxis(dt, 1, 0), jnp.moveaxis(u, 1, 0), jnp.moveaxis(Bm, 1, 0), jnp.moveaxis(Cm, 1, 0))
            _, ys = jax.lax.scan(step, h0, xs)
            y = jnp.moveaxis(ys, 0, 1) + u * Dp
            y = y * jax.nn.silu(z)
            return jnp.einsum('bld,ed->ble', y, Wout)
        key = jax.random.key(seed)
        kx, kf, kb = jax.random.split(key, 3)
        inp = {'x': jax.random.normal(kx, (BATCH, SEQ, D_MODEL), jnp.float32), 'norm_g': jnp.ones((D_MODEL,), jnp.float32), 'norm_b': jnp.zeros((D_MODEL,), jnp.float32)}
        for pfx, k in (('f', kf), ('b', kb)):
            for name, v in _mamba_params(k).items():
                inp[f'{pfx}_{name}'] = v
        return inp
    _L0_attn_in = _L0_attn_setup()

    def _L0_ffn_setup():
        import jax, jax.numpy as jnp
        import numpy as np
        HIDDEN = 256
        HEAD_DIM = 64
        N_EXPERTS = 16
        MIN_EXPERTS = 2
        B, T = (4, 512)

        def _normalize(x, axis):
            n = jnp.sqrt(jnp.sum(x * x, axis=axis, keepdims=True))
            return x / jnp.maximum(n, 1e-12)

        def _ste(x):
            hard = jax.lax.stop_gradient((x > 0).astype(x.dtype))
            return hard + x - jax.lax.stop_gradient(x)

        def _gating(hidden_states, sim_matrix, gates):
            b, t, c = hidden_states.shape
            flat = hidden_states.reshape(b * t, c)
            logits = _normalize(flat, -1) @ _normalize(sim_matrix, 0) - jax.nn.sigmoid(gates)
            gated = jax.nn.relu(logits)
            mask = _ste(gated)
            inactive = jnp.sum(mask, axis=1) == 0
            _, fb_idx = jax.lax.top_k(logits, MIN_EXPERTS)
            fb = jnp.zeros_like(mask).at[jnp.arange(b * t)[:, None], fb_idx].set(1.0)
            fb_applied = inactive[:, None] & (fb > 0)
            mask = jnp.where(fb_applied, 1.0, mask)
            masked_logits = jnp.where(mask > 0, gated, -jnp.inf)
            return jax.nn.softmax(masked_logits, axis=-1).reshape(b, t, -1)
        key = jax.random.key(seed)
        ks = jax.random.split(key, 6)
        xav_qkv = float(np.sqrt(6.0 / (HIDDEN + HEAD_DIM)))
        return {'hidden_states': jax.random.normal(ks[0], (B, T, HIDDEN), dtype=jnp.float32), 'sim_matrix': jax.random.normal(ks[1], (HIDDEN, N_EXPERTS), dtype=jnp.float32), 'gates': jnp.zeros((N_EXPERTS,), dtype=jnp.float32), 'q_proj': jax.random.uniform(ks[2], (N_EXPERTS, HIDDEN, HEAD_DIM), jnp.float32, -xav_qkv, xav_qkv), 'k_proj': jax.random.uniform(ks[3], (N_EXPERTS, HIDDEN, HEAD_DIM), jnp.float32, -xav_qkv, xav_qkv), 'v_proj': jax.random.uniform(ks[4], (N_EXPERTS, HIDDEN, HEAD_DIM), jnp.float32, -xav_qkv, xav_qkv), 'o_proj': jax.random.uniform(ks[5], (N_EXPERTS, HEAD_DIM, HIDDEN), jnp.float32, -xav_qkv, xav_qkv)}
    _L0_ffn_in = _L0_ffn_setup()
    _L0_c = _w((lambda *s: np.random.randn(*s).astype(np.float32) * 0.05)(8, 256))
    _L0_wmod = _w((lambda *s: np.random.randn(*s).astype(np.float32) * 0.05)(256, 6 * 256) * 256 ** (-0.5))
    _d = {'L0_attn_x': _L0_attn_in['x'], 'L0_attn_norm_g': _L0_attn_in['norm_g'], 'L0_attn_norm_b': _L0_attn_in['norm_b'], 'L0_attn_f_Win': _L0_attn_in['f_Win'], 'L0_attn_f_convw': _L0_attn_in['f_convw'], 'L0_attn_f_convb': _L0_attn_in['f_convb'], 'L0_attn_f_Wx': _L0_attn_in['f_Wx'], 'L0_attn_f_Wdt': _L0_attn_in['f_Wdt'], 'L0_attn_f_bdt': _L0_attn_in['f_bdt'], 'L0_attn_f_Alog': _L0_attn_in['f_Alog'], 'L0_attn_f_D': _L0_attn_in['f_D'], 'L0_attn_f_Wout': _L0_attn_in['f_Wout'], 'L0_attn_b_Win': _L0_attn_in['b_Win'], 'L0_attn_b_convw': _L0_attn_in['b_convw'], 'L0_attn_b_convb': _L0_attn_in['b_convb'], 'L0_attn_b_Wx': _L0_attn_in['b_Wx'], 'L0_attn_b_Wdt': _L0_attn_in['b_Wdt'], 'L0_attn_b_bdt': _L0_attn_in['b_bdt'], 'L0_attn_b_Alog': _L0_attn_in['b_Alog'], 'L0_attn_b_D': _L0_attn_in['b_D'], 'L0_attn_b_Wout': _L0_attn_in['b_Wout'], 'L0_ffn_sim_matrix': _L0_ffn_in['sim_matrix'], 'L0_ffn_gates': _L0_ffn_in['gates'], 'L0_ffn_q_proj': _L0_ffn_in['q_proj'], 'L0_ffn_k_proj': _L0_ffn_in['k_proj'], 'L0_ffn_v_proj': _L0_ffn_in['v_proj'], 'L0_ffn_o_proj': _L0_ffn_in['o_proj'], 'L0_c': _L0_c, 'L0_wmod': _L0_wmod}
    _x0 = _d['L0_attn_x']
    _d['L0_attn_x'] = jax.random.normal(jax.random.fold_in(jax.random.key(seed), 1), (8, 1024, 256), dtype=_x0.dtype)
    del _x0
    return _d

def reference(L0_attn_x, L0_attn_norm_g, L0_attn_norm_b, L0_attn_f_Win, L0_attn_f_convw, L0_attn_f_convb, L0_attn_f_Wx, L0_attn_f_Wdt, L0_attn_f_bdt, L0_attn_f_Alog, L0_attn_f_D, L0_attn_f_Wout, L0_attn_b_Win, L0_attn_b_convw, L0_attn_b_convb, L0_attn_b_Wx, L0_attn_b_Wdt, L0_attn_b_bdt, L0_attn_b_Alog, L0_attn_b_D, L0_attn_b_Wout, L0_ffn_sim_matrix, L0_ffn_gates, L0_ffn_q_proj, L0_ffn_k_proj, L0_ffn_v_proj, L0_ffn_o_proj, L0_c, L0_wmod):

    def _L0_attn_ref(x, norm_g, norm_b, f_Win, f_convw, f_convb, f_Wx, f_Wdt, f_bdt, f_Alog, f_D, f_Wout, b_Win, b_convw, b_convb, b_Wx, b_Wdt, b_bdt, b_Alog, b_D, b_Wout):
        import jax, jax.numpy as jnp
        import numpy as np
        D_MODEL = 256
        D_STATE = 16
        D_CONV = 4
        EXPAND = 2
        D_INNER = EXPAND * D_MODEL
        DT_RANK = (D_MODEL + 15) // 16
        BATCH = 2
        SEQ = 512
        EPS = 1e-05

        def _mamba_params(key, scale=0.02):
            ks = jax.random.split(key, 8)
            n = lambda k, s: jax.random.normal(k, s, jnp.float32) * scale
            return {'Win': n(ks[0], (2 * D_INNER, D_MODEL)), 'convw': n(ks[1], (D_INNER, 1, D_CONV)), 'convb': n(ks[2], (D_INNER,)), 'Wx': n(ks[3], (DT_RANK + 2 * D_STATE, D_INNER)), 'Wdt': n(ks[4], (D_INNER, DT_RANK)), 'bdt': n(ks[5], (D_INNER,)), 'Alog': jnp.log(jnp.tile(jnp.arange(1, D_STATE + 1, dtype=jnp.float32), (D_INNER, 1))), 'D': jnp.ones((D_INNER,), jnp.float32), 'Wout': n(ks[6], (D_MODEL, D_INNER))}

        def _mamba(x, Win, convw, convb, Wx, Wdt, bdt, Alog, Dp, Wout):
            B, L, _ = x.shape
            xz = jnp.einsum('bld,ed->ble', x, Win)
            u, z = jnp.split(xz, 2, axis=-1)
            uc = jnp.transpose(u, (0, 2, 1))
            uc = jnp.pad(uc, ((0, 0), (0, 0), (D_CONV - 1, 0)))
            uc = jax.lax.conv_general_dilated(uc, convw, (1,), 'VALID', feature_group_count=D_INNER)
            uc = uc + convb[None, :, None]
            u = jax.nn.silu(jnp.transpose(uc, (0, 2, 1)))
            xdbl = jnp.einsum('bld,ed->ble', u, Wx)
            dtr, Bm, Cm = jnp.split(xdbl, [DT_RANK, DT_RANK + D_STATE], axis=-1)
            dt = jax.nn.softplus(jnp.einsum('blr,dr->bld', dtr, Wdt) + bdt)
            A = -jnp.exp(Alog)

            def step(h, ins):
                dt_t, u_t, B_t, C_t = ins
                h = jnp.exp(dt_t[..., None] * A) * h + (dt_t * u_t)[..., None] * B_t[:, None, :]
                y_t = jnp.einsum('bdn,bn->bd', h, C_t)
                return (h, y_t)
            h0 = jnp.zeros((B, D_INNER, D_STATE), jnp.float32)
            xs = (jnp.moveaxis(dt, 1, 0), jnp.moveaxis(u, 1, 0), jnp.moveaxis(Bm, 1, 0), jnp.moveaxis(Cm, 1, 0))
            _, ys = jax.lax.scan(step, h0, xs)
            y = jnp.moveaxis(ys, 0, 1) + u * Dp
            y = y * jax.nn.silu(z)
            return jnp.einsum('bld,ed->ble', y, Wout)
        mu = jnp.mean(x, axis=-1, keepdims=True)
        var = jnp.var(x, axis=-1, keepdims=True)
        xn = (x - mu) * jax.lax.rsqrt(var + EPS) * norm_g + norm_b
        y_fwd = _mamba(xn, f_Win, f_convw, f_convb, f_Wx, f_Wdt, f_bdt, f_Alog, f_D, f_Wout)
        y_bwd = _mamba(jnp.flip(xn, axis=1), b_Win, b_convw, b_convb, b_Wx, b_Wdt, b_bdt, b_Alog, b_D, b_Wout)
        y_bwd = jnp.flip(y_bwd, axis=1)
        return x + y_fwd + y_bwd

    def _L0_ffn_ref(hidden_states, sim_matrix, gates, q_proj, k_proj, v_proj, o_proj):
        import jax, jax.numpy as jnp
        import numpy as np
        HIDDEN = 256
        HEAD_DIM = 64
        N_EXPERTS = 16
        MIN_EXPERTS = 2
        B, T = (4, 512)

        def _normalize(x, axis):
            n = jnp.sqrt(jnp.sum(x * x, axis=axis, keepdims=True))
            return x / jnp.maximum(n, 1e-12)

        def _ste(x):
            hard = jax.lax.stop_gradient((x > 0).astype(x.dtype))
            return hard + x - jax.lax.stop_gradient(x)

        def _gating(hidden_states, sim_matrix, gates):
            b, t, c = hidden_states.shape
            flat = hidden_states.reshape(b * t, c)
            logits = _normalize(flat, -1) @ _normalize(sim_matrix, 0) - jax.nn.sigmoid(gates)
            gated = jax.nn.relu(logits)
            mask = _ste(gated)
            inactive = jnp.sum(mask, axis=1) == 0
            _, fb_idx = jax.lax.top_k(logits, MIN_EXPERTS)
            fb = jnp.zeros_like(mask).at[jnp.arange(b * t)[:, None], fb_idx].set(1.0)
            fb_applied = inactive[:, None] & (fb > 0)
            mask = jnp.where(fb_applied, 1.0, mask)
            masked_logits = jnp.where(mask > 0, gated, -jnp.inf)
            return jax.nn.softmax(masked_logits, axis=-1).reshape(b, t, -1)
        b, t, c = hidden_states.shape
        rw = _gating(hidden_states, sim_matrix, gates)
        q = jnp.einsum('bte,bted->btd', rw, jnp.einsum('btc,ecd->bted', hidden_states, q_proj))
        k = jnp.einsum('bte,bted->btd', rw, jnp.einsum('btc,ecd->bted', hidden_states, k_proj))
        v = jnp.einsum('bte,bted->btd', rw, jnp.einsum('btc,ecd->bted', hidden_states, v_proj))
        scale = 1.0 / jnp.sqrt(jnp.asarray(HEAD_DIM, dtype=q.dtype))
        scores = jnp.einsum('bqd,bkd->bqk', q, k) * scale
        causal = jnp.tril(jnp.ones((t, t), dtype=bool))
        scores = jnp.where(causal, scores, -jnp.inf)
        attn = jnp.einsum('bqk,bkd->bqd', jax.nn.softmax(scores, axis=-1), v)
        mixed = attn[:, :, None, :] * rw[..., None]
        return jnp.einsum('bted,edc->btc', mixed, o_proj)
    x = L0_attn_x
    mod = (_silu(L0_c) @ L0_wmod).reshape(L0_c.shape[0], 6, 1, -1)
    sa, ca, ga, sb, cb, gb = (mod[:, 0], mod[:, 1], mod[:, 2], mod[:, 3], mod[:, 4], mod[:, 5])
    ga = (2 * (ga >= 0) - 1) * jnp.maximum(jnp.abs(ga), 0.25)
    gb = (2 * (gb >= 0) - 1) * jnp.maximum(jnp.abs(gb), 0.25)
    h = _layernorm(x, axis=-1) * (1 + ca) + sa
    x = x + ga * _L0_attn_ref(h, L0_attn_norm_g, L0_attn_norm_b, L0_attn_f_Win, L0_attn_f_convw, L0_attn_f_convb, L0_attn_f_Wx, L0_attn_f_Wdt, L0_attn_f_bdt, L0_attn_f_Alog, L0_attn_f_D, L0_attn_f_Wout, L0_attn_b_Win, L0_attn_b_convw, L0_attn_b_convb, L0_attn_b_Wx, L0_attn_b_Wdt, L0_attn_b_bdt, L0_attn_b_Alog, L0_attn_b_D, L0_attn_b_Wout)
    h = _layernorm(x, axis=-1) * (1 + cb) + sb
    x = x + gb * _L0_ffn_ref(h, L0_ffn_sim_matrix, L0_ffn_gates, L0_ffn_q_proj, L0_ffn_k_proj, L0_ffn_v_proj, L0_ffn_o_proj)
    return x

_drawn_inputs = setup_inputs


def setup_inputs(seed=0):
    import zlib

    import numpy as np

    out = dict(_drawn_inputs(seed))
    spreads = {'L0_attn_norm_g': (1.0, 0.6),
     'L0_attn_norm_b': (0.0, 0.8),
     'L0_attn_f_D': (1.0, 0.6),
     'L0_attn_b_D': (1.0, 0.6),
     'L0_ffn_gates': (0.0, 2.0)}
    factors = {'L0_attn_f_Win': 8.0,
     'L0_attn_f_convw': 8.0,
     'L0_attn_f_convb': 8.0,
     'L0_attn_f_Wx': 8.0,
     'L0_attn_f_Wdt': 8.0,
     'L0_attn_f_bdt': 8.0,
     'L0_attn_f_Alog': 8.0,
     'L0_attn_f_Wout': 8.0,
     'L0_attn_b_Win': 8.0,
     'L0_attn_b_convw': 8.0,
     'L0_attn_b_convb': 8.0,
     'L0_attn_b_Wx': 8.0,
     'L0_attn_b_Wdt': 8.0,
     'L0_attn_b_bdt': 8.0,
     'L0_attn_b_Alog': 8.0,
     'L0_attn_b_Wout': 8.0,
     'L0_ffn_sim_matrix': 33.393,
     'L0_ffn_q_proj': 51.901,
     'L0_ffn_k_proj': 51.726,
     'L0_ffn_v_proj': 32.125,
     'L0_ffn_o_proj': 31.993}
    for name, (base, spread) in spreads.items():
        noise = np.random.default_rng([zlib.crc32(name.encode()), seed]).standard_normal(out[name].shape)
        drawn = base * np.exp(spread * noise) if base else spread * noise
        out[name] = jnp.asarray(drawn.astype(out[name].dtype))
    for name, factor in factors.items():
        out[name] = (out[name] * factor).astype(out[name].dtype)
    return out
```

```python
from contextlib import ExitStack

import concourse.bass as bass
from concourse import mybir

F32 = mybir.dt.float32
ALU = mybir.AluOpType
ACT = mybir.ActivationFunctionType
AX = mybir.AxisListType.X

P = 128
B, L, D = 8, 1024, 256
DI, NS, NTAP, RANK = 512, 16, 4, 16
NE, HD = 16, 64
KD = D // P
J = DI // P
UL = 512
UT = UL // P
NT = L // P
NU = 4
STEPS = NU * NS
EC = 2
NCH = NE // EC
QW = 3 * HD
R_DT, R_B, R_C, XR = (0, 32), (32, 0), 64, 80
EPS = 1e-5
BIG = 1e30
RING = 4
SIDE = 3


PER = {
    "p_T": 4, "U": 16, "V": 16, "W": 16, "X": 4, "C": 4, "D": 16, "Z": 16, "yT": 16, "yo": 16,
    "l_T": 4, "l_lg": 1, "q": 32, "a_T": 4, "S": 8, "PT": 8, "PV": 8, "OT": 8, "FO": 8,
}


def banks_of(stage, k):
    if stage not in PER:
        return 0
    if stage in ("q", "OT"):
        return 2
    if stage in ("S", "PT"):
        return 1 if k < 4 else 2
    return 1


TABLE = """
# unit 0
 0| bl:3.0- yT:3.0- bl:3.1- yT:3.1-
 1| bl:3.2- bl:3.3- yT:3.2- yo:3.0- yo:3.1- yT:3.3- yo:3.2- dg:1.0 yo:3.3- l_ld- U:1.0 l_st-
 2| l_pw- U:1.1 Z:0.0 l_n.0-
 3| V:1.0 l_h.0- l_h.1- Z:0.1 l_n.1- l_h.2- l_T.0- l_h.3-
 4| l_T.1- l_T.2- dg:1.1 U:1.2 l_T.3- bl:0.0 l_sq- Z:0.2
 5| l_rn- V:1.1 dg:1.2 l_lg- U:1.3 V:1.2
 6| dg:1.3 V:1.3 l_ge- l_gt- w_ld.0- q.0-
 7| q.1- dg:1.4
 8| q.2- sl:1
 9| g_ld X:1
10| D:1.0 D:1.1
11| D:1.2 D:1.3 W:1.0
12| sp:1 q.3- w_ld.1-
13| Z:0.3 q.4- ad:1.0 W:1.1 dm:1.0 ad:1.1
14| C:1 q.5- W:1.2 dm:1.1 ad:1.2
15| dm:1.2 ad:1.3 zs:0 W:1.3 dm:1.3 q.6-
# unit 1
 0| dg:2.0 q.7- U:2.0
 1| U:2.1 w_ld.2- q.8- yT:0.0
 2| bl:0.1 yo:0.0 bl:0.2 yT:0.1 yT:0.2
 3| V:2.0 q.9-
 4| yo:0.1 dg:2.1 q.10-
 5| U:2.2 q.11- bl:0.3 V:2.1 w_ld.3- q.12-
 6| dg:2.2 U:2.3 q.13-
 7| q.14- V:2.2 q.15- yT:0.3 w_ld.4- dg:2.3
 8| q.16- V:2.3 dg:2.4 sl:2 q.17-
 9| Z:1.0 q.18- X:2
10| q.19- D:2.0 w_ld.5-
11| D:2.1 q.20- D:2.2
12| D:2.3 yo:0.2 sp:2 q.21- yo:0.3 q.22- W:2.0
13| ad:2.0 C:2 dm:2.0 q.23- Z:1.1 ad:2.1 bl:1.0
14| W:2.1 W:2.2 dm:2.1 w_ld.6- W:2.3 ad:2.2 q.24- Z:1.2
15| dm:2.2 q.25- ad:2.3 bl:1.1 dm:2.3
# unit 2
 0| Z:1.3 zs:1 q.26- yT:1.0
 1| q.27- w_ld.7- yo:1.0 yT:1.1 q.28- bl:1.2 yT:1.2
 2| yo:1.1 bl:1.3 q.29- yo:1.2 yT:1.3
 3| q.30- Z:2.0
 4| yo:1.3 dg:3.0 q.31-
 5| a_T.0- a_T.1- a_T.2- a_T.3- Z:2.1 S.0- E.0- U:3.0 U:3.1 PT.0- V:3.0 PV.0-
 6| M.0- OT.0- S.1- dg:3.1
 7| E.1- FO.0- PT.1- U:3.2 PV.1- M.1-
 8| OT.1- V:3.1 bl:2.0 S.2-
 9| FO.1- E.2- dg:3.2 PT.2- U:3.3 PV.2- M.2- V:3.2 OT.2- S.3- dg:3.3
10| FO.2- E.3- PT.3- V:3.3 PV.3- M.3- dg:3.4 sl:3
11| OT.3- X:3 S.4-
12| E.4- D:3.0 D:3.1 D:3.2 D:3.3 sp:3 FO.3- Z:2.2 PT.4- W:3.0 C:3 PV.4-
13| M.4- ad:3.0 OT.4- Z:2.3 dm:3.0 ad:3.1 dm:3.1 S.5-
14| E.5- ad:3.2 FO.4- PT.5- W:3.1 dm:3.2 PV.5- ad:3.3 bl:2.1 W:3.2 M.5-
15| OT.5- W:3.3 S.6- dm:3.3
# unit 3
 0| FO.5- E.6- zs:2 PT.6- PV.6- M.6-
 1| OT.6- FO.6- S.7- yT:2.0
 2| E.7- PT.7- PV.7- yT:2.1
 3| M.7- OT.7-
 4| FO.7- x_ld+
 5| p_st+
 6| p_pw+ p_n.0+
 7| p_h.0+ p_h.1+ bl:2.2 yo:2.0 p_n.1+ p_h.2+ p_h.3+ bl:2.3 yT:2.2 yo:2.1 p_st2+ p_pw2+ Z:3.0 p_base.0+
  | p_base.1+ yT:2.3 Z:3.1 Z:3.2 Z:3.3 zs:3 p_base.2+ p_base.3+ p_xn.0+ yo:2.2 p_T.0+ p_T.1+ p_xn.1+
 8| p_T.2+ p_T.3+ dg:0.0+ U:0.0+ U:0.1+ V:0.0+ dg:0.1+
 9| U:0.2+ V:0.1+ dg:0.2+ U:0.3+ V:0.2+
10| dg:0.3+ V:0.3+
11| dg:0.4+ sl:0+
12| X:0+
13| D:0.0+ D:0.1+ D:0.2+ D:0.3+ sp:0+ W:0.0+
14| W:0.1+ ad:0.0+ dm:0.0+ W:0.2+ W:0.3+ ad:0.1+
15| dm:0.1+ ad:0.2+ dm:0.2+ ad:0.3+ C:0+ dm:0.3+ yo:2.3
"""


def spread(text):
    steps = []
    for line in text.splitlines():
        head, bar, row = line.partition("|")
        if not bar:
            continue
        if head.strip():
            steps.append([])
        for w in row.split():
            db = {"+": 1, "-": -1}.get(w[-1], 0)
            name, _dot, k = w.rstrip("+-").partition(".")
            st, _colon, s = name.partition(":")
            steps[-1].append((st, db, int(s or 0), int(k or 0)))
    assert len(steps) == STEPS, len(steps)
    return steps


def plan():
    every = spread(TABLE)
    flat = [p for step in every for p in step]
    rows = {
        "prologue": [[p for p in flat if p[1] == 1]],
        "first": [[p for p in step if p[1] >= 0] for step in every],
        "steady": every,
        "last": [[p for p in step if p[1] <= 0] for step in every],
        "epilogue": [[p for p in flat if p[1] == -1]],
    }
    out, tenants = {}, [None] * SIDE
    for name, steps in rows.items():
        tenants = [t and (t[0], t[1] - 1, t[2], t[3]) for t in tenants]
        at_start, made = list(tenants), []
        turn = -sum(banks_of(p[0], p[3]) for step in steps for p in step) % SIDE
        for step in steps:
            row = []
            for p in step:
                got = []
                for _ in range(banks_of(p[0], p[3])):
                    got.append((turn % SIDE, tenants[turn % SIDE]))
                    tenants[turn % SIDE] = p
                    turn += 1
                row.append((p, got))
            made.append(row)
        if name == "steady":
            again = [t and (t[0], t[1] - 1, t[2], t[3]) for t in tenants]
            assert again == at_start, "a loop's turn must find the banks as the turn before it left them"
        out[name] = made
    return out


def done(b, per, i):
    return b * per + (i + 1)


def need(eng, sem, value):
    if isinstance(value, int) and value <= 0:
        return
    eng.wait_ge(sem, value)


def unit(s):
    back, half = s // 2, s % 2
    return back, half, (UL * half if not back else L - UL * (half + 1))


def tile_of(s, k):
    back, half, _ = unit(s)
    return NT - 1 - (UT * half + k) if back else UT * half + k


def program(nc, a, out, mod_d, hy_d):
    with ExitStack() as ctx:
        used = {}

        def sb(name, shape, dt=F32):
            n = 4
            for x in shape[1:]:
                n *= x
            used[name] = n
            return ctx.enter_context(nc.sbuf_tensor(name, shape, dt))

        win = [sb(f"win{i}", [P, KD, 2 * DI]) for i in range(2)]
        wx = [sb(f"wx{i}", [P, J, XR]) for i in range(2)]
        wdt2 = sb("wdt2", [R_DT[1] + RANK, DI])
        wdt = [wdt2[r:r + RANK, :] for r in R_DT]
        wout = [sb(f"wout{i}", [P, J, D]) for i in range(2)]
        convw = [sb(f"convw{i}", [P, J, NTAP]) for i in range(2)]
        vecs = [sb(f"vecs{i}", [P, 3, J]) for i in range(2)]
        aneg = [sb(f"aneg{i}", [P, J, NS]) for i in range(2)]
        norm = sb("norm", [P, 2, KD])
        wexp = sb("wexp", [P, NE * HD // P, D])
        simn = sb("simn", [P, KD, NE])
        sgate = sb("sgate", [P, NE])
        rank = sb("rank", [P, NE])
        ident = sb("ident", [P, P])
        causal = sb("causal", [P, P])
        mhalf = sb("mhalf", [P, NE])
        zero3 = sb("zero3", [P, NTAP - 1])
        one = sb("one", [P, 1])
        decay = sb("decay", [P, RING, UL])
        binp = sb("binp", [P, RING, UL])
        hst = sb("hst", [P, 2, J, UL])
        acc = sb("acc", [P, 2, UT, DI])
        bbc = sb("bbc", [P, 2, UL])
        carry = sb("carry", [P, J, NS])
        upad = sb("upad", [P, 2, UL + NTAP - 1])
        halo = sb("halo", [P, J, NTAP - 1])
        diag = sb("diag", [P, NTAP, P])
        us = sb("us", [P, J, UL])
        dtb = sb("dtb", [P, 2, J, UL])
        dub = sb("dub", [P, 2, J, UL])
        xd = sb("xd", [XR, 2, UL])
        ct = sb("ct", [P, 2, UT, NS])
        sz = sb("sz", [P, J, UL])
        yg = sb("yg", [P, 2, J, P])
        ytmp = sb("ytmp", [P, D])
        hyt = sb("hyt", [P, 2, D])
        ga_bc = sb("ga_bc", [P, D])
        xnT = sb("xnT", [P, KD, L])
        bufx = sb("bufx", [P, NT, D])
        bufh = sb("bufh", [P, NT, D])
        x2f = sb("x2f", [P, NT, D])
        h2T = sb("h2T", [P, KD, L])
        modp = sb("modp", [P, 3, D])
        modl = sb("modl", [P, 2, D])
        gb_bc = sb("gb_bc", [P, D])
        stx = sb("stx", [P, NT, 6])
        mvx = sb("mvx", [P, NT, 2])
        mvh = sb("mvh", [P, NT, 2])
        mvl = sb("mvl", [P, NT, 2])
        rsx = sb("rsx", [P, 4, NT])
        ve = sb("ve", [P, 4, NT])
        rw = sb("rw", [P, NT, NE])
        attn = sb("attn", [P, HD])
        small = sb("small", [P, 4, NT])
        mxs = sb("mxs", [P, 4])
        rsum = sb("rsum", [P, 2])
        ft = sb("ft", [P, 2, D])

        basetmp = ft[:]
        qkvb = bufh[:].rearrange("p a b -> p (a b)")[:, 0:NT * QW].rearrange("p (t c) -> p t c", t=NT)
        xflat = bufx[:].rearrange("p a b -> p (a b)")
        prob, probT = xflat[:, 0:L], xflat[:, L:2 * L].rearrange("p (k t) -> p k t", k=NT)
        qkT = h2T
        wo = wexp
        wq = wexp[:].rearrange("p a b -> p (a b)")[:, 0:2 * KD * EC * QW].rearrange("p (a k n) -> p a k n", a=2, k=KD)
        gt = [xflat[:, P * i:P * (i + 1)].rearrange("p (t e) -> p t e", t=NT) for i in range(6)]
        junk = xflat[:, L:2 * L].bitcast(mybir.dt.bfloat16).rearrange("p (t c) -> p t c", t=NT)
        cT = us[:, 0, 0:KD * B].rearrange("p (k b) -> p k b", k=KD)
        wmod = hst[:].rearrange("p a j t -> p (a j t)")[:, 0:KD * 6 * D].rearrange("p (k n) -> p k n", k=KD)
        mods = x2f[:].rearrange("p a b -> p (a b)")[0:B, 0:6 * D].rearrange("p (m c) -> p m c", m=6)
        simraw = us[:, 1, 0:KD * NE].rearrange("p (k e) -> p k e", k=KD)
        simsq = us[:, 2, 0:KD * NE].rearrange("p (k e) -> p k e", k=KD)
        simrn = us[:, 3, 0:NE]
        ones = sz[:, 0, 0:P]
        gsgn = [sz[0:B, 1, 0:D], sz[0:B, 2, 0:D]]

        hT = [ctx.enter_context(nc.psum_tensor(f"hT{i}", [P, 512], F32)) for i in range(UT)]
        bps = ctx.enter_context(nc.psum_tensor("bps", [P, 512], F32))
        side = [ctx.enter_context(nc.psum_tensor(f"side{i}", [P, 512], F32)) for i in range(SIDE)]

        sems = {}

        def sem(name):
            if name not in sems:
                sems[name] = ctx.enter_context(nc.semaphore(name))
            return sems[name]

        s_w, s_mods, s_modst = sem("weights_in"), sem("mods_ready"), sem("mods_stored")
        s_x, s_modp, s_modl = sem("x_in"), sem("modp_in"), sem("modl_in")
        s_ga, s_gb, s_base = sem("ga_in"), sem("gb_in"), sem("base_stored")
        s_hyl = [sem("partial_in0"), sem("partial_in1")]
        s_hys = [sem("partial_stored0"), sem("partial_stored1")]
        s_wq = [sem("wq_in0"), sem("wq_in1")]
        s_wo = sem("wo_in")
        s_out = [sem("out_stored0"), sem("out_stored1")]
        s_bp, s_bc, s_dec, s_in = sem("b_spread"), sem("b_copied"), sem("decay_ready"), sem("input_ready")
        s_scan, s_turn, s_acc, s_car = sem("scanned"), sem("state_turned"), sem("readout_added"), sem("carried")
        pe_ = {st: sem(f"pe_{st}") for st in PER}
        tk_ = {st: sem(f"took_{st}") for st in PER}
        s_stx, s_aggx, s_pwv, s_pw, s_pn = sem("stx"), sem("aggx"), sem("pw_var"), sem("pw"), sem("normed_x")
        s_ph1, s_ph, s_sth, s_aggh = sem("scaled_x"), sem("mod_x"), sem("sth"), sem("aggh")
        s_pw2v, s_pw2, s_pb1, s_pb, s_pxn = sem("pw2_var"), sem("pw2"), sem("gated_h"), sem("base"), sem("normed_h")
        s_dg, s_sl, s_sp0, s_sp1, s_ad, s_dm = (sem("diag"), sem("silu_u"), sem("softplus_exp"), sem("softplus_ln"),
                                                sem("dt"), sem("dtu"))
        s_zs, s_yadd = sem("silu_z"), sem("unit_out")
        s_stl, s_aggl, s_pw3v, s_pw3, s_ln = sem("stl"), sem("aggl"), sem("pw3_var"), sem("pw3"), sem("normed_2")
        s_lh1, s_lh, s_sq, s_rn1, s_rn = sem("scaled_2"), sem("mod_2"), sem("squares"), sem("rn_pow"), sem("rn")
        s_gate, s_gexp, s_gate2 = sem("gate_step"), sem("gate_exp"), sem("gate_norm")
        s_qst, s_s, s_exp, s_ri, s_mix, s_fadd = (sem("expert_added"), sem("score_step"), sem("prob"), sem("rsum_inv"),
                                                  sem("mixed"), sem("final"))
        s_c, s_pc, s_ac, s_vc, s_pec = (sem("consts"), sem("pool_once"), sem("act_once"), sem("dve_once"),
                                        sem("pe_once"))
        NGATE = 22
        tk_["l_lg"] = s_gate

        def wait_apart(eng, *waits):
            waits = [(sm, v if isinstance(v, int) else eng.compute_val(v)) for sm, v in waits]
            eng.wait_ge(s_c, 1)
            for sm, v in waits:
                need(eng, sm, v)

        def holder(tenant, b):
            if tenant is None:
                return s_c, 1
            st, db, s, k = tenant
            if st in ("U", "V", "W", "D", "Z", "yT", "yo"):
                k = 4 * s + k
            elif st in ("X", "C"):
                k = s
            if st == "q":
                return s_qst, done(b + db, 4 * PER[st], 4 * k + 3)
            per = NGATE if st == "l_lg" else PER[st]
            return tk_[st], done(b + db, per, k)

        PLAN = plan()
        WEIGHTS = []

        def walk(eng, stages, core, flush):
            def pieces(row, b, seg):
                for (st, db, s, k), got in row:
                    if st in stages:
                        stages[st](b + db, s, k, [side[i] for i, _ in got], [(t, b) for _, t in got], seg)

            def body(b, seg):
                for i, row in enumerate(PLAN[seg]):
                    core(b, i // NS, i % NS, seg)
                    pieces(row, b, seg)

            pieces(PLAN["prologue"][0], -1, "prologue")
            core(-1, NU - 1, NS, "prologue")
            body(0, "first")
            with eng.Fori(1, B - 1) as b:
                body(b, "steady")
            body(B - 1, "last")
            flush()
            pieces(PLAN["epilogue"][0], B, "epilogue")

        block = ctx.enter_context(nc.Block())

        @block.sync
        def _(sp):
            n = 0
            pairs = []
            for i, d in enumerate("fb"):
                pairs += [(win[i][:], a[f"win_{d}"]), (wdt[i], a[f"wdt_{d}"]), (wout[i][:], a[f"wout_{d}"]),
                          (convw[i][:], a[f"convw_{d}"]), (vecs[i][:], a[f"vecs_{d}"]),
                          (aneg[i][:], a[f"alog_{d}"])]
            pairs += [(norm[:], a["norm"]), (simraw, a["sim"]), (cT, a["cT"]), (wmod, a["wmod"]),
                      (sgate[:], a["gates"].partition_broadcast(P)), (rank[:], a["rank"].partition_broadcast(P))]
            for dst, src in pairs:
                sp.dma_start(dst, src).then_inc(s_w, 16)
                n += 16
            sp.wait_ge(s_pc, 1)
            for i, d in enumerate("fb"):
                for r, c in ((R_DT[i], 0), (R_B[i], RANK), (R_C, RANK + NS)):
                    sp.dma_start(wx[i][:, :, r:r + NS], a[f"wx_{d}"][:, :, c:c + NS]).then_inc(s_w, 16)
                    n += 16
            WEIGHTS.append(n)
            sp.wait_ge(s_mods, 1)
            sp.dma_start(mod_d, mods).then_inc(s_modst, 16)
            sp.wait_ge(s_modst, 16)

            def row(b, m0, m1):
                return mod_d[bass.ds(b, 1), m0:m1, :].partition_broadcast(P).rearrange("p a m c -> p (a m) c")

            def tokens(t, b):
                return t[bass.ds(b, 1), :, :].rearrange("a (t p) c -> p (a t) c", p=P)

            def token_tile(t, b, k):
                return t[bass.ds(b, 1), k * P:(k + 1) * P, :].rearrange("a p c -> p (a c)")

            def x_ld(b, s, k, *_):
                need(sp, pe_["FO"], done(b - 2, PER["FO"], NT - 1))
                need(sp, s_base, (b) * 16)
                sp.dma_start(bufx[:], tokens(a["x"], b)).then_inc(s_x, 16)
                need(sp, s_pb, done(b - 1, 4, 3))
                sp.dma_start(modp[:], row(b, 0, 3)).then_inc(s_modp, 16)

            def p_base(b, s, k, *_):
                if k == 3:
                    need(sp, s_pb, done(b, 4, 3))
                    sp.dma_start(tokens(hy_d, b), bufx[:]).then_inc(s_base, 16)

            def g_ld(b, s, k, *_):
                need(sp, tk_["yo"], done(b - 1, PER["yo"], 15))
                sp.dma_start(ga_bc[:], row(b, 2, 3).rearrange("p m c -> p (m c)")).then_inc(s_ga, 16)

            def bl(b, s, k, *_):
                back, half, _0 = unit(s)
                waits = [(s_yadd, done(b, 16, 4 * s + k - 2))]
                if back:
                    waits += [(x, 16 * done(b, 4, 3)) for x in s_hys]
                else:
                    waits += [(s_base, (b + 1) * 16), (s_hys[k % 2], 16 * done(b, 4, 2 * s + k // 2 - 1))]
                wait_apart(sp, *waits)
                sp.dma_start(hyt[:, k % 2, :], token_tile(hy_d, b, tile_of(s, k))).then_inc(s_hyl[k % 2], 16)

            def yo(b, s, k, *_):
                if not unit(s)[0]:
                    need(sp, s_yadd, done(b, 16, 4 * s + k))
                    sp.dma_start(token_tile(hy_d, b, tile_of(s, k)), hyt[:, k % 2, :]).then_inc(s_hys[k % 2], 16)

            def l_ld(b, s, k, *_):
                sp.dma_start(modl[:], row(b, 3, 5)).then_inc(s_modl, 16)
                sp.dma_start(gb_bc[:], row(b, 5, 6).rearrange("p m c -> p (m c)")).then_inc(s_gb, 16)

            def w_ld(b, s, g, *_):
                if g >= 2:
                    need(sp, pe_["q"], done(b, 32, 4 * (g - 2) + 3))
                sp.dma_start(wq[:, g % 2], a["wqkv"][g]).then_inc(s_wq[g % 2], 16)

            def a_T(b, s, k, *_):
                if k == 0:
                    need(sp, pe_["q"], done(b, 32, 31))
                    sp.dma_start(wo[:], a["wo"]).then_inc(s_wo, 16)

            def FO(b, s, k, *_):
                need(sp, s_fadd, done(b, 8, k))
                sp.dma_start(token_tile(out, b, k), ft[:, k % 2, :]).then_inc(s_out[k % 2], 16)

            walk(sp, {"x_ld": x_ld, "p_base": p_base, "g_ld": g_ld, "bl": bl, "yo": yo, "l_ld": l_ld,
                      "w_ld": w_ld, "a_T": a_T, "FO": FO}, lambda *_: None, lambda: None)
            for q in range(2):
                sp.wait_ge(s_out[q], 16 * B * NT // 2)
                sp.wait_ge(s_hys[q], 16 * B * 4)

        @block.tensor
        def _(pe):
            def take(tenants):
                for t, b in tenants:
                    need(pe, *holder(t, b))

            pe.wait_ge(s_w, WEIGHTS[0])
            pe.wait_ge(s_c, 1)
            pe.wait_ge(s_ac, 2)
            for m in range(3):
                for k in range(KD):
                    mm = pe.matmul(hT[m][0:B, :], cT[:, k, :], wmod[:, k, 512 * m:512 * (m + 1)],
                                   start=(k == 0), stop=(k == KD - 1))
            for k in range(KD):
                mm = pe.matmul(hT[3][:, 0:NE], ones, simsq[:, k, :], start=(k == 0), stop=(k == KD - 1))
            mm.then_inc(s_pec, 1)

            def p_T(b, s, i, bk, tn, seg):
                take(tn)
                need(pe, s_pxn, done(b, 2, i // 2))
                for k in range(KD):
                    for q in range(2):
                        mm = pe.transpose(bk[0][:, 256 * k + P * q:256 * k + P * (q + 1)],
                                          bufh[:, 2 * i + q, k * P:(k + 1) * P], ident[:])
                mm.then_inc(pe_["p_T"], 1)

            def U(b, s, j, bk, tn, seg):
                back, half, lo = unit(s)
                take(tn)
                need(pe, tk_["p_T"], done(b, 4, 3))
                for k in range(KD):
                    x = xnT[:, k, lo:lo + UL]
                    mm = pe.matmul(bk[0][:], win[back][:, k, j * P:(j + 1) * P], x[:, ::-1] if back else x,
                                   start=(k == 0), stop=(k == KD - 1))
                mm.then_inc(pe_["U"], 1)

            def V(b, s, j, bk, tn, seg):
                take(tn)
                need(pe, tk_["U"], done(b, 16, 4 * s + j))
                need(pe, s_dg, done(b, 20, 5 * s + j))
                for k in range(NTAP):
                    mm = pe.matmul(bk[0][:], diag[:, k, :], upad[:, j % 2, k:k + UL], start=(k == 0),
                                   stop=(k == NTAP - 1))
                mm.then_inc(pe_["V"], 1)

            def W(b, s, j, bk, tn, seg):
                take(tn)
                need(pe, s_sl, done(b, 4, s))
                need(pe, s_dg, done(b, 20, 5 * s + 4))
                for t in range(UT):
                    mm = pe.matmul(bk[0][:, t * P:(t + 1) * P], us[:, j, t * P:(t + 1) * P], diag[:, j, :],
                                   start=True, stop=True)
                mm.then_inc(pe_["W"], 1)

            def X(b, s, _k, bk, tn, seg):
                take(tn)
                need(pe, s_sl, done(b, 4, s))
                for j in range(J):
                    mm = pe.matmul(bk[0][0:XR, :], wx[s // 2][:, j, :], us[:, j, :], start=(j == 0), stop=(j == J - 1))
                mm.then_inc(pe_["X"], 1)

            def C(b, s, _k, bk, tn, seg):
                wait_apart(pe, holder(*tn[0]), (tk_["X"], done(b, 4, s)))
                for t in range(UT):
                    mm = pe.transpose(bk[0][:, t * NS:(t + 1) * NS], xd[R_C:R_C + NS, s % 2, t * P:(t + 1) * P],
                                      ident[R_C:R_C + NS, R_C:R_C + NS])
                mm.then_inc(pe_["C"], 1)

            def Dt(b, s, j, bk, tn, seg):
                take(tn)
                need(pe, tk_["X"], done(b, 4, s))
                r = R_DT[s // 2]
                pe.matmul(bk[0][:], wdt[s // 2][:, j * P:(j + 1) * P], xd[r:r + RANK, s % 2, :],
                          start=True, stop=True).then_inc(pe_["D"], 1)

            def Z(b, s, j, bk, tn, seg):
                back, half, lo = unit(s)
                take(tn)
                need(pe, tk_["p_T"], done(b, 4, 3))
                for k in range(KD):
                    mm = pe.matmul(bk[0][:], win[back][:, k, DI + j * P:DI + (j + 1) * P], xnT[:, k, lo:lo + UL],
                                   start=(k == 0), stop=(k == KD - 1))
                mm.then_inc(pe_["Z"], 1)

            def yT(b, s, k, bk, tn, seg):
                take(tn)
                need(pe, s_acc, done(b, 4 * STEPS, 4 * NS * s + 4 * NS - 1))
                for j in range(J):
                    mm = pe.transpose(bk[0][:, j * P:(j + 1) * P], acc[:, s % 2, k, j * P:(j + 1) * P], ident[:])
                mm.then_inc(pe_["yT"], 1)

            def yo(b, s, k, bk, tn, seg):
                take(tn)
                need(pe, tk_["yT"], done(b, 16, 4 * s + k))
                for j in range(J):
                    mm = pe.matmul(bk[0][:, 0:D], yg[:, k % 2, j, :], wout[s // 2][:, j, :], start=(j == 0),
                                   stop=(j == J - 1))
                mm.then_inc(pe_["yo"], 1)

            def l_T(b, s, i, bk, tn, seg):
                take(tn)
                need(pe, s_lh, done(b, 4, i))
                for k in range(KD):
                    for q in range(2):
                        mm = pe.transpose(bk[0][:, 256 * k + P * q:256 * k + P * (q + 1)],
                                          bufh[:, 2 * i + q, k * P:(k + 1) * P], ident[:])
                mm.then_inc(pe_["l_T"], 1)

            def l_lg(b, s, _k, bk, tn, seg):
                take(tn)
                need(pe, tk_["l_T"], done(b, 4, 3))
                for t in range(NT):
                    for k in range(KD):
                        mm = pe.matmul(bk[0][:, t * NE:(t + 1) * NE], h2T[:, k, t * P:(t + 1) * P], simn[:, k, :],
                                       start=(k == 0), stop=(k == KD - 1))
                mm.then_inc(pe_["l_lg"], 1)

            def q(b, s, i, bk, tn, seg):
                g, pair = i // 4, i % 4
                take(tn)
                need(pe, s_wq[g % 2], 16 * done(b, 4, g // 2))
                for h in range(2):
                    t = 2 * pair + h
                    for k in range(KD):
                        mm = pe.matmul(bk[h][:, 0:EC * QW], h2T[:, k, t * P:(t + 1) * P], wq[:, g % 2, k, :],
                                       start=(k == 0), stop=(k == KD - 1))
                mm.then_inc(pe_["q"], 1)

            def a_T(b, s, i, bk, tn, seg):
                wait_apart(pe, holder(*tn[0]), (s_qst, done(b, 128, 127)))
                for w in range(2):
                    for h in range(2):
                        mm = pe.transpose(bk[0][0:HD, 256 * w + P * h:256 * w + P * (h + 1)],
                                          qkvb[:, 2 * i + h, w * HD:(w + 1) * HD], ident[:])
                mm.then_inc(pe_["a_T"], 1)

            def S(b, s, i, bk, tn, seg):
                take(tn)
                need(pe, tk_["a_T"], done(b, 4, 3))
                for h in range(len(bk)):
                    w = min((i + 1) * P - 512 * h, 512)
                    mm = pe.matmul(bk[h][:, 0:w], qkT[0:HD, 0, i * P:(i + 1) * P], qkT[0:HD, 1, 512 * h:512 * h + w],
                                   start=True, stop=True)
                mm.then_inc(pe_["S"], 1)

            def PT(b, s, i, bk, tn, seg):
                take(tn)
                need(pe, s_exp, done(b, 8, i))
                for k in range(i + 1):
                    mm = pe.transpose(bk[k // 4][:, (k % 4) * P:(k % 4 + 1) * P], prob[:, k * P:(k + 1) * P], ident[:])
                mm.then_inc(pe_["PT"], 1)

            def PV(b, s, i, bk, tn, seg):
                take(tn)
                need(pe, tk_["PT"], done(b, 8, i))
                for k in range(i + 1):
                    mm = pe.matmul(bk[0][:, 0:HD], probT[:, k, :], qkvb[:, k, 2 * HD:3 * HD], start=(k == 0),
                                   stop=(k == i))
                mm.then_inc(pe_["PV"], 1)

            def OT(b, s, i, bk, tn, seg):
                take(tn)
                need(pe, s_mix, done(b, 8, i))
                for k in range(NT):
                    mm = pe.transpose(bk[k // 4][:, (k % 4) * P:(k % 4 + 1) * P], prob[:, k * P:(k + 1) * P], ident[:])
                mm.then_inc(pe_["OT"], 1)

            def FO(b, s, i, bk, tn, seg):
                take(tn)
                need(pe, tk_["OT"], done(b, 8, i))
                need(pe, s_wo, 16 * (b + 1))
                for k in range(NT):
                    mm = pe.matmul(bk[0][:, 0:D], probT[:, k, :], wo[:, k, :], start=(k == 0), stop=(k == NT - 1))
                mm.then_inc(pe_["FO"], 1)

            def turn(b, i):
                need(pe, s_scan, done(b, 4 * STEPS, 4 * i + 3))
                for t in range(UT):
                    need(pe, s_acc, done(b, 4 * STEPS, 4 * (i - 1) + t))
                    for j in range(J):
                        mm = pe.transpose(hT[t][:, j * P:(j + 1) * P], hst[:, i % 2, j, t * P:(t + 1) * P], ident[:])
                    mm.then_inc(s_turn, 1)

            def core(b, s, n, seg):
                i = NS * s + n
                nxt = i + 1 if seg != "prologue" else i
                if not (seg == "last" and nxt == STEPS):
                    m, r = nxt % NS, R_B[nxt // NS % NU // 2]
                    need(pe, tk_["X"], done(b, 4, nxt // NS))
                    need(pe, s_bc, done(b, STEPS, nxt - 1))
                    pe.matmul(bps[:], ident[r:r + NS, r + m:r + m + 1].to_broadcast([NS, P]),
                              xd[r:r + NS, (nxt // NS) % 2, :], start=True, stop=True).then_inc(s_bp, 1)
                if seg != "prologue" and not (seg == "first" and i == 0):
                    turn(b, i - 1)

            pe.wait_ge(s_vc, 9)
            pe.wait_ge(s_ac, 3)
            walk(pe, {"p_T": p_T, "U": U, "V": V, "W": W, "X": X, "C": C, "D": Dt, "Z": Z, "yT": yT, "yo": yo,
                      "l_T": l_T, "l_lg": l_lg, "q": q, "a_T": a_T, "S": S, "PT": PT, "PV": PV, "OT": OT, "FO": FO},
                 core, lambda: turn(B - 1, STEPS - 1))

        @block.scalar
        def _(act):
            act.wait_ge(s_w, WEIGHTS[0])
            act.wait_ge(s_pc, 2)
            act.activation(cT, cT, ACT.Silu).then_inc(s_ac, 1)
            act.activation(simsq, simraw, ACT.Square).then_inc(s_ac, 1)
            act.activation(sgate[:], sgate[:], ACT.Sigmoid)
            for i in range(2):
                ins = act.activation(aneg[i][:], aneg[i][:], ACT.Exp)
            ins.then_inc(s_ac, 1)

            def p_T(b, s, i, bk, tn, seg):
                act.wait_ge(pe_["p_T"], done(b, 4, i))
                for k in range(KD):
                    ins = act.activation(xnT[:, k, 256 * i:256 * (i + 1)], bk[0][:, 256 * k:256 * (k + 1)], ACT.Identity,
                                         bias=norm[:, 1, k:k + 1], scale=norm[:, 0, k:k + 1])
                ins.then_inc(tk_["p_T"], 1)

            def U(b, s, j, bk, tn, seg):
                half = s % 2
                act.wait_ge(pe_["U"], done(b, 16, 4 * s + j))
                act.activation(upad[:, j % 2, 0:NTAP - 1], halo[:, j, :] if half else zero3[:], ACT.Copy)
                if not half:
                    act.activation(halo[:, j, :], bk[0][:, UL - NTAP + 1:UL], ACT.Copy)
                act.activation(upad[:, j % 2, NTAP - 1:], bk[0][:], ACT.Copy).then_inc(tk_["U"], 1)

            def V(b, s, j, bk, tn, seg):
                act.wait_ge(pe_["V"], done(b, 16, 4 * s + j))
                need(act, s_dm, done(b, 16, 4 * s - 1))
                act.activation(us[:, j, :], bk[0][:], ACT.Identity, bias=vecs[s // 2][:, 0, j:j + 1])\
                   .then_inc(tk_["V"], 1)

            def sl(b, s, k, bk, tn, seg):
                act.wait_ge(tk_["V"], done(b, 16, 4 * s + 3))
                act.activation(us[:], us[:], ACT.Silu).then_inc(s_sl, 1)

            def W(b, s, j, bk, tn, seg):
                act.wait_ge(pe_["W"], done(b, 16, 4 * s + j))
                need(act, pe_["yT"], done(b, 16, 4 * s - 5))
                act.activation(acc[:, s % 2, :, j * P:(j + 1) * P], bk[0][:].rearrange("p (t d) -> p t d", t=UT),
                               ACT.Copy).then_inc(tk_["W"], 1)

            def X(b, s, k, bk, tn, seg):
                act.wait_ge(pe_["X"], done(b, 4, s))
                act.activation(xd[:, s % 2, :], bk[0][0:XR, :], ACT.Copy).then_inc(tk_["X"], 1)

            def C(b, s, k, bk, tn, seg):
                act.wait_ge(pe_["C"], done(b, 4, s))
                need(act, s_acc, done(b, 4 * STEPS, 4 * NS * (s - 1) - 1))
                act.activation(ct[:, s % 2].rearrange("p t n -> p (t n)"), bk[0][:, 0:UT * NS], ACT.Copy)\
                   .then_inc(tk_["C"], 1)

            def Dt(b, s, j, bk, tn, seg):
                bias = vecs[s // 2][:, 1, j:j + 1]
                act.wait_ge(pe_["D"], done(b, 16, 4 * s + j))
                need(act, s_in, done(b, 4 * STEPS, 4 * NS * (s - 1) - 1))
                act.activation(dtb[:, s % 2, j, :], bk[0][:], ACT.Abs, bias=bias)
                act.activation(dub[:, s % 2, j, :], bk[0][:], ACT.Relu, bias=bias).then_inc(tk_["D"], 1)

            def sp_(b, s, k, bk, tn, seg):
                v = dtb[:, s % 2]
                act.wait_ge(tk_["D"], done(b, 16, 4 * s + 3))
                act.activation(v, v, ACT.Exp, scale=-1.0).then_inc(s_sp0, 1)
                act.wait_ge(s_sp0, done(b, 4, s))
                act.activation(v, v, ACT.Ln, bias=one[:, 0:1]).then_inc(s_sp1, 1)

            def Z(b, s, j, bk, tn, seg):
                act.wait_ge(pe_["Z"], done(b, 16, 4 * s + j))
                need(act, tk_["yT"], done(b, 16, 4 * s - 1))
                act.activation(sz[:, j, :], bk[0][:], ACT.Copy).then_inc(tk_["Z"], 1)

            def zs(b, s, k, bk, tn, seg):
                act.wait_ge(tk_["Z"], done(b, 16, 4 * s + 3))
                act.activation(sz[:], sz[:], ACT.Silu).then_inc(s_zs, 1)

            def l_T(b, s, i, bk, tn, seg):
                act.wait_ge(pe_["l_T"], done(b, 4, i))
                act.activation(h2T[:, :, 256 * i:256 * (i + 1)], bk[0][:].rearrange("p (k t) -> p k t", k=KD),
                               ACT.Copy).then_inc(tk_["l_T"], 1)

            def l_sq(b, s, k, bk, tn, seg):
                act.wait_ge(s_lh, done(b, 4, 3))
                act.wait_ge(s_base, 16 * (b + 2) if seg != "epilogue" else 16 * B)
                for t in range(NT):
                    ins = act.activation(junk[:, t, :], bufh[:, t, :], ACT.Square, accum_out=ve[:, 3, t:t + 1])
                ins.then_inc(s_sq, 1)

            def l_ge(b, s, k, bk, tn, seg):
                act.wait_ge(s_gate, done(b, NGATE, NGATE - 1))
                act.activation(gt[0], gt[0], ACT.Exp).then_inc(s_gexp, 1)

            def a_T(b, s, i, bk, tn, seg):
                act.wait_ge(pe_["a_T"], done(b, 4, i))
                act.activation(qkT[0:HD, :, 256 * i:256 * (i + 1)], bk[0][0:HD, :].rearrange("p (k t) -> p k t", k=2),
                               ACT.Copy).then_inc(tk_["a_T"], 1)

            def E(b, s, i, bk, tn, seg):
                act.wait_ge(tk_["S"], done(b, 8, i))
                v = prob[:, 0:(i + 1) * P]
                act.activation(v, v, ACT.Exp, bias=mxs[:, 3:4], scale=HD ** -0.5, accum_out=rsum[:, 0:1])\
                   .then_inc(s_exp, 1)

            def PT(b, s, i, bk, tn, seg):
                act.wait_ge(pe_["PT"], done(b, 8, i))
                for h in range(len(bk)):
                    w = min(i + 1 - 4 * h, 4)
                    ins = act.activation(probT[:, 4 * h:4 * h + w, :],
                                         bk[h][:, 0:w * P].rearrange("p (k t) -> p k t", k=w), ACT.Copy)
                ins.then_inc(tk_["PT"], 1)

            def OT(b, s, i, bk, tn, seg):
                act.wait_ge(pe_["OT"], done(b, 8, i))
                for h in range(2):
                    ins = act.activation(probT[:, 4 * h:4 * h + 4, :], bk[h][:].rearrange("p (k t) -> p k t", k=4),
                                         ACT.Copy)
                ins.then_inc(tk_["OT"], 1)

            def core(b, s, n, seg):
                i = NS * s + n
                nxt = i + 1 if seg != "prologue" else i
                if seg != "prologue":
                    if n == 0:
                        act.wait_ge(s_ad, done(b, 16, 4 * s + 3))
                    for j in range(J):
                        r = 4 * i + j
                        need(act, s_scan, done(b, 4 * STEPS, r - RING))
                        act.activation(decay[:, r % RING, :], dtb[:, s % 2, j, :], ACT.Exp,
                                       scale=aneg[s // 2][:, j, n:n + 1]).then_inc(s_dec, 1)
                if not (seg == "last" and nxt == STEPS):
                    act.wait_ge(s_bp, done(b, STEPS, nxt))
                    need(act, s_in, done(b, 4 * STEPS, 4 * (nxt - 2) + 3))
                    act.activation(bbc[:, nxt % 2, :], bps[:], ACT.Copy).then_inc(s_bc, 1)

            walk(act, {"p_T": p_T, "U": U, "V": V, "sl": sl, "W": W, "X": X, "C": C, "D": Dt, "sp": sp_, "Z": Z,
                       "zs": zs, "l_T": l_T, "l_sq": l_sq, "l_ge": l_ge, "a_T": a_T, "E": E, "PT": PT, "OT": OT},
                 core, lambda: None)

        @block.gpsimd
        def _(pool):
            for i in range(2):
                ins = pool.memset(wx[i][:], 0.0)
            ins.then_inc(s_pc, 1)
            pool.memset(ident[:], 0.0)
            pool.memset(causal[:], 0.0)
            pool.memset(zero3[:], 0.0)
            pool.memset(ones, 1.0)
            pool.memset(mhalf[:], -0.5)
            pool.memset(one[:], 1.0).then_inc(s_pc, 1)
            pool.wait_ge(s_pc, 2)
            pool.affine_select(out=ident[:], in_=ident[:], compare_op=ALU.not_equal, fill=1.0, base=0,
                               pattern=[[-1, P]], channel_multiplier=1)
            pool.affine_select(out=causal[:], in_=causal[:], compare_op=ALU.is_ge, fill=-BIG, base=0,
                               pattern=[[-1, P]], channel_multiplier=1).then_inc(s_c, 1)
            pool.wait_ge(s_ac, 3)
            for i in range(2):
                ins = pool.tensor_scalar(aneg[i][:], aneg[i][:], -1.0, None, ALU.mult)
            ins.then_inc(s_pc, 1)
            pool.wait_ge(s_vc, 1)
            pool.tensor_tensor(simrn, simrn, mhalf[:], ALU.pow).then_inc(s_pc, 1)
            pool.wait_ge(s_pc, 4)
            pool.tensor_scalar(simrn, simrn, 1e12, None, ALU.min).then_inc(s_pc, 1)
            pool.wait_ge(s_pc, 5)
            pool.tensor_tensor(simn[:], simraw, simrn.unsqueeze(1).broadcast_to([P, KD, NE]), ALU.mult)\
                .then_inc(s_pc, 1)
            pool.wait_ge(s_vc, 9)

            def power(mv, w, b, s_in_, s_mid, s_end):
                wait_apart(pool, (s_in_, done(b, 1, 0)))
                pool.tensor_scalar(ve[:, w, :], mv[:, :, 1], EPS, None, ALU.add).then_inc(s_mid, 1)
                pool.wait_ge(s_mid, done(b, 1, 0))
                pool.tensor_tensor(rsx[:, w, :], ve[:, w, :], mhalf[:, 0:NT], ALU.pow).then_inc(s_end, 1)

            def p_pw(b, *_):
                power(mvx, 0, b, s_aggx, s_pwv, s_pw)

            def p_pw2(b, *_):
                power(mvh, 1, b, s_aggh, s_pw2v, s_pw2)

            def l_pw(b, *_):
                power(mvl, 2, b, s_aggl, s_pw3v, s_pw3)

            def modulate(b, i, mod, s_mid, s_end):
                v = bufh[:, 2 * i:2 * i + 2, :]
                pool.tensor_tensor(v, v, mod[:, 1:2, :].broadcast_to([P, 2, D]), ALU.mult).then_inc(s_mid, 1)
                pool.wait_ge(s_mid, done(b, 4, i))
                pool.tensor_tensor(v, v, mod[:, 0:1, :].broadcast_to([P, 2, D]), ALU.add).then_inc(s_end, 1)

            def p_h(b, s, i, *_):
                pool.wait_ge(s_pn, done(b, 2, i // 2))
                pool.wait_ge(s_modp, 16 * (b + 1))
                modulate(b, i, modp, s_ph1, s_ph)

            def p_base(b, s, i, *_):
                v = bufx[:, 2 * i:2 * i + 2, :]
                if i == 0:
                    for q in range(2):
                        need(pool, s_out[q], 16 * done(b - 2, 4, 3))
                else:
                    pool.wait_ge(s_pb, done(b, 4, i - 1))
                pool.tensor_tensor(basetmp, bufh[:, 2 * i:2 * i + 2, :], modp[:, 2:3, :].broadcast_to([P, 2, D]),
                                   ALU.mult).then_inc(s_pb1, 1)
                pool.wait_ge(s_pb1, done(b, 4, i))
                pool.tensor_tensor(v, v, basetmp, ALU.add).then_inc(s_pb, 1)

            def dg(b, s, j, *_):
                back = s // 2
                if j == 0:
                    need(pool, tk_["W"], done(b, 16, 4 * s - 1))
                else:
                    need(pool, tk_["V"], done(b, 16, 4 * s + j - 1))
                w = convw[back][:, j, :] if j < J else vecs[back][:, 2, :]
                pool.tensor_tensor(diag[:], ident[:].unsqueeze(1).broadcast_to([P, NTAP, P]),
                                   w.unsqueeze(2).broadcast_to([P, NTAP, P]), ALU.mult).then_inc(s_dg, 1)

            def ad(b, s, j, *_):
                pool.wait_ge(s_sp1, done(b, 4, s))
                pool.tensor_tensor(dtb[:, s % 2, j, :], dtb[:, s % 2, j, :], dub[:, s % 2, j, :], ALU.add)\
                    .then_inc(s_ad, 1)

            def dm(b, s, j, *_):
                pool.wait_ge(s_ad, done(b, 16, 4 * s + j))
                pool.tensor_tensor(dub[:, s % 2, j, :], dtb[:, s % 2, j, :], us[:, j, :], ALU.mult).then_inc(s_dm, 1)

            def yo(b, s, k, *_):
                back = s // 2
                pool.wait_ge(tk_["yo"], done(b, 16, 4 * s + k))
                pool.wait_ge(s_hyl[k % 2], 16 * done(b, 8, 2 * s + k // 2))
                dst = x2f[:, tile_of(s, k), :] if back else hyt[:, k % 2, :]
                pool.tensor_tensor(dst, hyt[:, k % 2, :], ytmp[:], ALU.add).then_inc(s_yadd, 1)

            def l_h(b, s, i, *_):
                pool.wait_ge(s_ln, done(b, 2, i // 2))
                pool.wait_ge(s_modl, 16 * (b + 1))
                modulate(b, i, modl, s_lh1, s_lh)

            def l_rn(b, *_):
                pool.wait_ge(s_sq, done(b, 1, 0))
                pool.tensor_tensor(rsx[:, 3, :], ve[:, 3, :], mhalf[:, 0:NT], ALU.pow).then_inc(s_rn1, 1)
                wait_apart(pool, (s_rn1, done(b, 1, 0)))
                pool.tensor_scalar(rsx[:, 3, :], rsx[:, 3, :], 1e12, None, ALU.min).then_inc(s_rn, 1)

            def M(b, s, i, *_):
                pool.wait_ge(tk_["PV"], done(b, 8, i))
                pool.tensor_tensor(prob.rearrange("p (e d) -> p e d", e=NE),
                                   attn[:].unsqueeze(1).broadcast_to([P, NE, HD]),
                                   rw[:, i, :].unsqueeze(2).broadcast_to([P, NE, HD]), ALU.mult).then_inc(s_mix, 1)

            def FO(b, s, i, *_):
                pool.wait_ge(tk_["FO"], done(b, 8, i))
                pool.tensor_tensor(ft[:, i % 2, :], ft[:, i % 2, :], x2f[:, i, :], ALU.add).then_inc(s_fadd, 1)

            def core(b, s, n, seg):
                if seg == "prologue":
                    return
                i = NS * s + n
                if n == 0:
                    pool.wait_ge(s_dm, done(b, 16, 4 * s + 3))
                pool.wait_ge(s_bc, done(b, STEPS, i))
                for j in range(J):
                    r = 4 * i + j
                    need(pool, s_scan, done(b, 4 * STEPS, r - RING))
                    pool.tensor_tensor(binp[:, r % RING, :], dub[:, s % 2, j, :], bbc[:, i % 2, :], ALU.mult)\
                        .then_inc(s_in, 1)

            walk(pool, {"p_pw": p_pw, "p_pw2": p_pw2, "l_pw": l_pw, "p_h": p_h, "p_base": p_base, "dg": dg, "ad": ad,
                        "dm": dm, "yo": yo, "l_h": l_h, "l_rn": l_rn, "M": M, "FO": FO}, core, lambda: None)

        @block.vector
        def _(dve):
            dve.wait_ge(s_pec, 1)
            dve.tensor_copy(simrn, hT[3][:, 0:NE]).then_inc(s_vc, 1)
            m6 = mods.rearrange("p m c -> p (m c)")
            for m in range(3):
                dve.tensor_copy(m6[:, 512 * m:512 * (m + 1)], hT[m][0:B, :])
            dve.tensor_scalar(gsgn[0], hT[1][0:B, 0:D], 0.0, 2.0, ALU.is_ge, ALU.mult)
            dve.tensor_scalar(gsgn[1], hT[2][0:B, D:2 * D], 0.0, 2.0, ALU.is_ge, ALU.mult).then_inc(s_vc, 1)
            dve.wait_ge(s_vc, 2)
            for q in range(2):
                ins = dve.tensor_scalar(gsgn[q], gsgn[q], -1.0, None, ALU.add)
            ins.then_inc(s_vc, 1)
            dve.wait_ge(s_vc, 3)
            for q, m in enumerate((2, 5)):
                ins = dve.tensor_tensor(mods[:, m, :], mods[:, m, :], gsgn[q], ALU.mult)
            ins.then_inc(s_vc, 1)
            dve.wait_ge(s_vc, 4)
            for q, m in enumerate((2, 5)):
                ins = dve.tensor_scalar(mods[:, m, :], mods[:, m, :], 0.25, None, ALU.max)
            ins.then_inc(s_vc, 1)
            dve.wait_ge(s_vc, 5)
            for q, m in enumerate((2, 5)):
                ins = dve.tensor_tensor(mods[:, m, :], mods[:, m, :], gsgn[q], ALU.mult)
            ins.then_inc(s_vc, 1)
            for m in (1, 4):
                ins = dve.tensor_scalar(mods[:, m, :], mods[:, m, :], 1.0, None, ALU.add)
            ins.then_inc(s_vc, 1)
            dve.wait_ge(s_vc, 7)
            dve.engine_nop().then_inc(s_mods, 1)
            dve.wait_ge(s_pc, 6)
            dve.engine_nop().then_inc(s_vc, 1)
            dve.wait_ge(s_modst, 16)
            dve.engine_nop().then_inc(s_vc, 1)

            def stats(src, mv, b, s_st, s_ag):
                for t in range(NT):
                    ins = dve.bn_stats(stx[:, t, :], src[:, t, :])
                ins.then_inc(s_st, 1)
                wait_apart(dve, (s_st, done(b, 1, 0)))
                for t in range(NT):
                    ins = dve.bn_aggr(mv[:, t, :], stx[:, t, :])
                ins.then_inc(s_ag, 1)

            def normalise(dst, src, mv, w, i, s_end):
                for t in range(4 * i, 4 * i + 4):
                    ins = dve.tensor_scalar(dst[:, t, :], src[:, t, :], mv[:, t, 0:1], rsx[:, w, t:t + 1],
                                            ALU.subtract, ALU.mult)
                ins.then_inc(s_end, 1)

            def p_st(b, *_):
                dve.wait_ge(s_x, 16 * (b + 1))
                stats(bufx, mvx, b, s_stx, s_aggx)

            def p_n(b, s, i, *_):
                dve.wait_ge(s_pw, done(b, 1, 0))
                need(dve, pe_["p_T"], done(b - 1, 4, 3))
                normalise(bufh, bufx, mvx, 0, i, s_pn)

            def p_st2(b, *_):
                dve.wait_ge(s_ph, done(b, 4, 3))
                stats(bufh, mvh, b, s_sth, s_aggh)

            def p_xn(b, s, i, *_):
                dve.wait_ge(s_pw2, done(b, 1, 0))
                dve.wait_ge(s_pb, done(b, 4, 2 * i + 1))
                normalise(bufh, bufh, mvh, 1, i, s_pxn)

            def yT(b, s, k, bk, *_):
                back, half, lo = unit(s)
                at = (tile_of(s, k) - lo // P) * P
                dve.wait_ge(pe_["yT"], done(b, 16, 4 * s + k))
                dve.wait_ge(s_zs, done(b, 4, s))
                need(dve, pe_["yo"], done(b, 16, 4 * s + k - 2))
                y = bk[0][:].rearrange("p (j t) -> p j t", j=J)
                dve.tensor_tensor(yg[:, k % 2], y[:, :, ::-1] if back else y, sz[:, :, at:at + P], ALU.mult)\
                   .then_inc(tk_["yT"], 1)

            def yo(b, s, k, bk, *_):
                dve.wait_ge(pe_["yo"], done(b, 16, 4 * s + k))
                need(dve, s_yadd, done(b, 16, 4 * s + k - 1))
                dve.wait_ge(s_ga, 16 * (b + 1))
                dve.tensor_tensor(ytmp[:], bk[0][:, 0:D], ga_bc[:], ALU.mult).then_inc(tk_["yo"], 1)

            def l_st(b, *_):
                dve.wait_ge(s_yadd, done(b, 16, 15))
                stats(x2f, mvl, b, s_stl, s_aggl)

            def l_n(b, s, i, bk, tn, seg):
                dve.wait_ge(s_pw3, done(b, 1, 0))
                dve.wait_ge(pe_["p_T"], 4 * B if seg == "epilogue" else done(b + 1, 4, 3))
                normalise(bufh, x2f, mvl, 2, i, s_ln)

            def l_lg(b, s, _k, bk, tn, seg):
                at = [0]

                def step(ins):
                    ins.then_inc(s_gate, 1)
                    dve.wait_ge(s_gate, done(b, NGATE, at[0]))
                    at[0] += 1

                def over(v):
                    return v.unsqueeze(2).broadcast_to([P, NT, NE])

                def experts(v):
                    return v.unsqueeze(1).broadcast_to([P, NT, NE])

                G, LG, ON, K, S1, S2 = gt
                m0, m1, m2 = small[:, 0, :], small[:, 1, :], small[:, 2, :]
                dve.wait_ge(pe_["l_lg"], done(b, 1, 0))
                dve.wait_ge(s_rn, done(b, 1, 0))
                dve.wait_ge(s_base, 16 * B if seg == "epilogue" else 16 * (b + 2))
                step(dve.tensor_tensor(LG, bk[0][:, 0:NT * NE].rearrange("p (t e) -> p t e", t=NT),
                                       over(rsx[:, 3, :]), ALU.mult))
                step(dve.tensor_tensor(LG, LG, experts(sgate[:]), ALU.subtract))
                step(dve.tensor_scalar(G, LG, 0.0, None, ALU.max))
                step(dve.tensor_scalar(ON, G, 0.0, None, ALU.is_gt))
                step(dve.tensor_reduce(m0, ON, AX, ALU.max))
                step(dve.tensor_scalar(m0, m0, -1.0, 1.0, ALU.mult, ALU.add))
                for src, pick in ((LG, S1), (S2, S2)):
                    step(dve.tensor_reduce(m1, src, AX, ALU.max))
                    step(dve.tensor_tensor(K, src, over(m1), ALU.is_equal))
                    step(dve.tensor_tensor(K, K, experts(rank[:]), ALU.mult))
                    step(dve.tensor_reduce(m2, K, AX, ALU.max))
                    step(dve.tensor_tensor(pick, K, over(m2), ALU.is_equal))
                    if pick is S1:
                        step(dve.scalar_tensor_tensor(S2, S1, -BIG, LG, ALU.mult, ALU.add))
                step(dve.tensor_tensor(S1, S1, S2, ALU.add))
                step(dve.tensor_tensor(S1, S1, over(m0), ALU.mult))
                step(dve.tensor_tensor(ON, ON, S1, ALU.max))
                step(dve.tensor_reduce(m1, G, AX, ALU.max))
                step(dve.tensor_tensor(G, G, over(m1), ALU.subtract))
                assert at[0] == NGATE, at

            def l_gt(b, s, _k, bk, tn, seg):
                G, ON, m1, m2 = gt[0], gt[2], small[:, 1, :], small[:, 2, :]
                dve.wait_ge(s_gexp, done(b, 1, 0))
                dve.tensor_tensor(G, G, ON, ALU.mult).then_inc(s_gate2, 1)
                dve.wait_ge(s_gate2, done(b, 4, 0))
                dve.tensor_reduce(m1, G, AX, ALU.add).then_inc(s_gate2, 1)
                dve.wait_ge(s_gate2, done(b, 4, 1))
                dve.reciprocal(m2, m1).then_inc(s_gate2, 1)
                dve.wait_ge(s_gate2, done(b, 4, 2))
                dve.tensor_tensor(rw[:], G, m2.unsqueeze(2).broadcast_to([P, NT, NE]), ALU.mult).then_inc(s_gate2, 1)
                dve.wait_ge(s_gate2, done(b, 4, 3))

            def q(b, s, i, bk, *_):
                g, pair = i // 4, i % 4
                dve.wait_ge(pe_["q"], done(b, 32, i))
                if i == 0:
                    dve.wait_ge(pe_["l_T"], done(b, 4, 3))
                    dve.wait_ge(s_sq, done(b, 1, 0))
                for e in range(EC):
                    for h in range(2):
                        t, ex = 2 * pair + h, EC * g + e
                        v, src, w = qkvb[:, t, :], bk[h][:, e * QW:(e + 1) * QW], rw[:, t, ex:ex + 1]
                        if ex == 0:
                            ins = dve.tensor_scalar(v, src, w, None, ALU.mult)
                        else:
                            dve.wait_ge(s_qst, done(b, 128, 4 * i + 2 * e + h - 2 if e else 4 * (i - 4) + 2 + h))
                            ins = dve.scalar_tensor_tensor(v, src, w, v, ALU.mult, ALU.add)
                        ins.then_inc(s_qst, 1)

            def S(b, s, i, bk, tn, seg):
                dve.wait_ge(pe_["S"], done(b, 8, i))
                if i:
                    dve.wait_ge(pe_["OT"], done(b, 8, i - 1))
                if i == 0:
                    dve.wait_ge(s_gate2, done(b, 4, 3))
                for h in range(len(bk)):
                    w = min(i * P - 512 * h, 512)
                    if w > 0:
                        dve.tensor_copy(prob[:, 512 * h:512 * h + w], bk[h][:, 0:w])
                o = (i * P) % 512
                dve.tensor_tensor(prob[:, i * P:(i + 1) * P], bk[-1][:, o:o + P], causal[:], ALU.add).then_inc(s_s, 1)
                dve.wait_ge(s_s, done(b, 16, 2 * i))
                dve.tensor_reduce(mxs[:, 2:3], prob[:, 0:(i + 1) * P], AX, ALU.max).then_inc(s_s, 1)
                dve.wait_ge(s_s, done(b, 16, 2 * i + 1))
                if i:
                    dve.wait_ge(s_exp, done(b, 8, i - 1))
                dve.tensor_scalar(mxs[:, 3:4], mxs[:, 2:3], -(HD ** -0.5), None, ALU.mult).then_inc(tk_["S"], 1)

            def PV(b, s, i, bk, tn, seg):
                dve.wait_ge(s_exp, done(b, 8, i))
                dve.reciprocal(rsum[:, 1:2], rsum[:, 0:1]).then_inc(s_ri, 1)
                dve.wait_ge(s_ri, done(b, 8, i))
                dve.wait_ge(pe_["PV"], done(b, 8, i))
                if i:
                    dve.wait_ge(s_mix, done(b, 8, i - 1))
                dve.tensor_scalar(attn[:], bk[0][:, 0:HD], rsum[:, 1:2], None, ALU.mult).then_inc(tk_["PV"], 1)

            def FO(b, s, i, bk, tn, seg):
                dve.wait_ge(pe_["FO"], done(b, 8, i))
                if i < 2:
                    dve.wait_ge(s_pb, 4 * B if seg == "epilogue" else done(b + 1, 4, 3))
                if i >= 2 or seg == "epilogue":
                    dve.wait_ge(s_out[i % 2], 16 * done(b, 4, i // 2 - 1))
                dve.wait_ge(s_gb, 16 * (b + 1))
                dve.tensor_tensor(ft[:, i % 2, :], bk[0][:, 0:D], gb_bc[:], ALU.mult).then_inc(tk_["FO"], 1)

            def read_out(b, i, t):
                s, n = i // NS if i >= 0 else NU - 1, i % NS
                dve.wait_ge(s_turn, done(b, 4 * STEPS, 4 * i + t))
                if n == 0:
                    dve.wait_ge(tk_["W"], done(b, 16, 4 * (i // NS) + 3))
                    dve.wait_ge(tk_["C"], done(b, 4, i // NS))
                need(dve, s_acc, done(b, 4 * STEPS, 4 * (i - 1) + t))
                dve.scalar_tensor_tensor(acc[:, s % 2, t, :], hT[t][:], ct[:, s % 2, t, n:n + 1], acc[:, s % 2, t, :],
                                         ALU.mult, ALU.add).then_inc(s_acc, 1)

            def core(b, s, n, seg):
                if seg == "prologue":
                    return
                i, half = NS * s + n, s % 2
                for j in range(J):
                    r = 4 * i + j
                    dve.wait_ge(s_dec, done(b, 4 * STEPS, r))
                    dve.wait_ge(s_in, done(b, 4 * STEPS, r))
                    if j == 0:
                        need(dve, s_turn, done(b, 4 * STEPS, 4 * (i - 2) + 3))
                        if half:
                            dve.wait_ge(s_car, done(b, 2 * NS, NS * (s // 2) + n))
                    first = carry[:, j, n:n + 1] if half else 0.0
                    dve.tensor_tensor_scan(hst[:, i % 2, j, :], decay[:, r % RING, :], binp[:, r % RING, :], first,
                                           ALU.mult, ALU.add).then_inc(s_scan, 1)
                    if not (seg == "first" and i == 0):
                        read_out(b, i - 1, j)
                if not half:
                    dve.wait_ge(s_scan, done(b, 4 * STEPS, 4 * i + 3))
                    dve.tensor_copy(carry[:, :, n], hst[:, i % 2, :, UL - 1]).then_inc(s_car, 1)

            walk(dve, {"p_st": p_st, "p_n": p_n, "p_st2": p_st2, "p_xn": p_xn, "yT": yT, "yo": yo, "l_st": l_st,
                       "l_n": l_n, "l_lg": l_lg, "l_gt": l_gt, "q": q, "S": S, "PV": PV, "FO": FO},
                 core, lambda: [read_out(B - 1, STEPS - 1, t) for t in range(UT)])


def kernel(**inputs):
    import numpy as np
    import concourse.bacc as bacc
    from concourse.bass_utils import run_bass_kernel_spmd

    g = {k: np.asarray(v) for k, v in inputs.items()}

    def blocks(w):
        return w.reshape(-1, P, w.shape[-1]).transpose(1, 0, 2)

    arr = {"x": g["L0_attn_x"]}
    for d in "fb":
        q = lambda name: g[f"L0_attn_{d}_{name}"]
        arr[f"win_{d}"] = blocks(q("Win").T)
        arr[f"wx_{d}"] = blocks(q("Wx").T)
        arr[f"wdt_{d}"] = q("Wdt").T
        arr[f"wout_{d}"] = blocks(q("Wout").T)
        arr[f"convw_{d}"] = blocks(q("convw").reshape(DI, NTAP))
        arr[f"vecs_{d}"] = np.stack([q("convb"), q("bdt"), q("D")]).reshape(3, J, P).transpose(2, 0, 1)
        arr[f"alog_{d}"] = blocks(q("Alog"))
    arr["norm"] = np.stack([g["L0_attn_norm_g"], g["L0_attn_norm_b"]]).reshape(2, KD, P).transpose(2, 0, 1)
    w = np.stack([g["L0_ffn_q_proj"], g["L0_ffn_k_proj"], g["L0_ffn_v_proj"]])
    arr["wqkv"] = w.reshape(3, NCH, EC, KD, P, HD).transpose(1, 4, 3, 2, 0, 5).reshape(NCH, P, KD, EC * QW)
    arr["wo"] = blocks(g["L0_ffn_o_proj"].reshape(NE * HD, D))
    arr["sim"] = blocks(g["L0_ffn_sim_matrix"])
    arr["gates"] = g["L0_ffn_gates"]
    arr["rank"] = np.arange(NE, 0, -1, dtype=np.float32)
    arr["cT"] = blocks(g["L0_c"].T)
    arr["wmod"] = blocks(g["L0_wmod"])
    arr = {k: np.ascontiguousarray(v) for k, v in arr.items()}

    nc = bacc.Bacc("TRN2", target_bir_lowering=False, num_devices=1)
    aps = {k: nc.dram_tensor(f"in_{k}", v.shape, F32, kind="ExternalInput").ap() for k, v in arr.items()}
    out = nc.dram_tensor("out", (B, L, D), F32, kind="ExternalOutput").ap()
    mod_d = nc.dram_tensor("mod_scratch", (B, 6, D), F32).ap()
    hy_d = nc.dram_tensor("partial_scratch", (B, L, D), F32).ap()
    program(nc, aps, out, mod_d, hy_d)
    r = run_bass_kernel_spmd(nc, [{f"in_{k}": v for k, v in arr.items()}], core_ids=[0])
    return r.results[0]["out"]
```

```python
from contextlib import ExitStack

import concourse.bass as bass
from concourse import mybir

F32 = mybir.dt.float32
BF16 = mybir.dt.bfloat16
ALU = mybir.AluOpType
ACT = mybir.ActivationFunctionType
AX = mybir.AxisListType.X

P = 128
B, L, D = 8, 1024, 256
DI, NS, NTAP, RANK = 512, 16, 4, 16
NE, HD = 16, 64
KD = D // P
J = DI // P
UL = 512
UT = UL // P
NT = L // P
NU = 4
STEPS = NU * NS
EC = 2
NCH = NE // EC
QW = 3 * HD
ROWS_OF = (("C", "B", "B", "dt", "dt", "B"), ("dt", "B", "B", "C", "C", "B"))
R_B = (16, 32, 80)
R_DT, R_C, XR = (64, 0), (0, 64), 96
EPS = 1e-5
BIG = 1e30
RING = 4
SIDE = 3


PER = {
    "p_T": 4, "U": 16, "V": 16, "W": 16, "X": 4, "C": 4, "D": 16, "Z": 16, "yT": 16, "yo": 16,
    "l_T": 4, "l_lg": 1, "q": 32, "a_T": 4, "S": 8, "PT": 8, "PV": 8, "OT": 8, "FO": 8,
}


def banks_of(stage, k):
    if stage not in PER:
        return 0
    if stage in ("q", "OT"):
        return 2
    if stage in ("S", "PT"):
        return 1 if k < 4 else 2
    return 1


TABLE = """
# unit 0
 0| bl:3.0- bl:3.1- dg:1.0 U:1.0 yT:3.0- bl:3.2- yT:3.1-
 1| bl:3.3- yo:3.0- yT:3.2- yo:3.1- yT:3.3- l_ld- yo:3.2- yo:3.3- l_st- Z:0.0
 2| l_pw- l_n.0- Z:0.1
 3| l_h.0- U:1.1 l_h.1- l_n.1- Z:0.2
 4| l_h.2- V:1.0
 5| l_T.0- l_h.3- l_T.1- l_T.2- dg:1.1 U:1.2
 6| l_T.3- l_sq- l_rn- V:1.1 l_lg- dg:1.2 U:1.3 V:1.2
 7| l_ge- dg:1.3 V:1.3
 8| g_ld l_gt- w_ld.0- dg:1.4 q.0- sl:1
 9| X:1 Xr:1 q.1- Xm:1 Xl:1
10| bl:0.0 D:1.0 D:1.1 D:1.2
11| D:1.3 q.2-
12| sp:1 q.3- C:1
13| ad:1.0 dm:1.0 w_ld.1- W:1.0 bl:0.1 ad:1.1 Z:0.3 q.4-
14| dm:1.1 W:1.1 W:1.2 ad:1.2 q.5-
15| dm:1.2 ad:1.3 zs:0 q.6- W:1.3 dm:1.3
# unit 1
 0| q.7- dg:2.0 U:2.0 w_ld.2-
 1| U:2.1 q.8- yT:0.0
 2| yo:0.0 q.9-
 3| V:2.0 q.10-
 4| dg:2.1 q.11- U:2.2
 5| w_ld.3- q.12- V:2.1 bl:0.2
 6| dg:2.2 U:2.3 q.13-
 7| V:2.2 q.14- dg:2.3 yT:0.1
 8| q.15- w_ld.4- V:2.3 dg:2.4 q.16- yT:0.2 sl:2
 9| X:2 q.17- yo:0.1 q.18- Xr:2 Xm:2 yo:0.2 bl:0.3 Xl:2 q.19- yT:0.3 w_ld.5-
10| D:2.0 D:2.1 D:2.2 yo:0.3 q.20- C:2
11| D:2.3 q.21-
12| sp:2 q.22- Z:1.0
13| W:2.0 W:2.1 ad:2.0 W:2.2 q.23- dm:2.0 w_ld.6- ad:2.1 bl:1.0
14| dm:2.1 q.24- ad:2.2 Z:1.1
15| W:2.3 dm:2.2 Z:1.2 q.25- ad:2.3 dm:2.3
# unit 2
 0| Z:1.3 zs:1 q.26- yT:1.0 dg:3.0
 1| U:3.0 q.27- bl:1.1 yT:1.1
 2| w_ld.7- U:3.1 yo:1.0 q.28- yo:1.1 q.29- bl:1.2
 3| yT:1.2 q.30-
 4| V:3.0 bl:1.3 q.31-
 5| a_T.0- a_T.1- a_T.2- a_T.3- S.0- yT:1.3
 6| E.0- dg:3.1 PT.0- U:3.2 Z:2.0 PV.0- S.1-
 7| M.0- OT.0- E.1- FO.0- PT.1- S.2- PV.1-
 8| M.1- V:3.1 dg:3.2 U:3.3 OT.1-
 9| FO.1- E.2- PT.2- V:3.2 PV.2- M.2- S.3- dg:3.3
10| OT.2- V:3.3 E.3- dg:3.4 FO.2- sl:3 PT.3- Z:2.1 PV.3-
11| X:3 Xr:3 M.3- Xm:3 yo:1.2 S.4- Xl:3
12| E.4- D:3.0 D:3.1 D:3.2 OT.3-
13| D:3.3 yo:1.3 sp:3 FO.3- PT.4- W:3.0 PV.4- ad:3.0 M.4- S.5-
14| dm:3.0 OT.4- ad:3.1 dm:3.1 E.5- ad:3.2 bl:2.0 Z:2.2 FO.4- dm:3.2 PT.5- PV.5- M.5- S.6-
15| ad:3.3 C:3 dm:3.3 E.6- OT.5- W:3.1 FO.5- W:3.2 PT.6- W:3.3 PV.6-
# unit 3
 0| Z:2.3 M.6- OT.6-
 1| zs:2 FO.6- S.7-
 2| E.7- PT.7- PV.7-
 3| M.7- OT.7- bl:2.1
 4| FO.7- yT:2.0 x_ld+ yT:2.1
 5| p_st+
 6| p_pw+ p_n.0+ bl:2.2 p_n.1+
 7| p_h.0+ p_h.1+ p_h.2+ yo:2.0 yT:2.2 p_st2.0+ bl:2.3 p_h.3+ yo:2.1 yT:2.3 p_st2.1+
 8| Z:3.0 p_pw2.0+ Z:3.1 p_pw2.1+ Z:3.2 dg:0.0+ p_xn.0+ Z:3.3 yo:2.2 zs:3 p_xn.1+ p_T.0+ p_T.1+ p_T.2+ p_base.0+
  | p_T.3+
 9| U:0.0+ U:0.1+ V:0.0+
10| dg:0.1+ U:0.2+ V:0.1+
11| dg:0.2+ U:0.3+ V:0.2+ dg:0.3+
12| V:0.3+ dg:0.4+ sl:0+
13| X:0+ W:0.0+ p_base.1+ Xr:0+ Xm:0+ Xl:0+
14| D:0.0+ D:0.1+ p_base.2+ D:0.2+ D:0.3+ sp:0+
15| p_base.3+ ad:0.0+ dm:0.0+ W:0.1+ ad:0.1+ dm:0.1+ C:0+ W:0.2+ ad:0.2+ W:0.3+ dm:0.2+ ad:0.3+ dm:0.3+ yo:2.3
"""


def spread(text):
    steps = []
    for line in text.splitlines():
        head, bar, row = line.partition("|")
        if not bar:
            continue
        if head.strip():
            steps.append([])
        for w in row.split():
            db = {"+": 1, "-": -1}.get(w[-1], 0)
            name, _dot, k = w.rstrip("+-").partition(".")
            st, _colon, s = name.partition(":")
            steps[-1].append((st, db, int(s or 0), int(k or 0)))
    assert len(steps) == STEPS, len(steps)
    return steps


def alone(pieces):
    order = {"S": -4, "E": -3, "PT": 0, "PV": 3, "M": 4, "OT": 5, "FO": 6}
    rest = [p for p in pieces if p[0] not in order]
    tiles = [p for p in pieces if p[0] in order]
    return rest + sorted(tiles, key=lambda p: (7 * p[3] + order[p[0]], p[0]))


def plan():
    every = spread(TABLE)
    flat = [p for step in every for p in step]
    rows = {
        "prologue": [[p for p in flat if p[1] == 1]],
        "first": [[p for p in step if p[1] >= 0] for step in every],
        "steady": every,
        "last": [[p for p in step if p[1] <= 0] for step in every],
        "epilogue": [alone([p for p in flat if p[1] == -1])],
    }
    out, tenants = {}, [None] * SIDE
    for name, steps in rows.items():
        tenants = [t and (t[0], t[1] - 1, t[2], t[3]) for t in tenants]
        at_start, made = list(tenants), []
        if name == "epilogue":
            tenants += ["scan"] * UT
        banks = len(tenants)
        turn = -sum(banks_of(p[0], p[3]) for step in steps for p in step) % banks
        turn = 0 if name == "epilogue" else turn
        for step in steps:
            row = []
            for p in step:
                got = []
                for _ in range(banks_of(p[0], p[3])):
                    got.append((turn % banks, tenants[turn % banks]))
                    tenants[turn % banks] = p
                    turn += 1
                row.append((p, got))
            made.append(row)
        if name == "steady":
            again = [t and (t[0], t[1] - 1, t[2], t[3]) for t in tenants]
            assert again == at_start, "a loop's turn must find the banks as the turn before it left them"
        out[name] = made
    return out


def done(b, per, i):
    return b * per + (i + 1)


def need(eng, sem, value):
    if isinstance(value, int) and value <= 0:
        return
    eng.wait_ge(sem, value)


def unit(s):
    back, half = s // 2, s % 2
    return back, half, (UL * half if not back else L - UL * (half + 1))


def tile_of(s, k):
    back, half, _ = unit(s)
    return NT - 1 - (UT * half + k) if back else UT * half + k


def program(nc, a, out, mod_d, hy_d):
    with ExitStack() as ctx:
        def sb(name, shape, dt=F32):
            return ctx.enter_context(nc.sbuf_tensor(name, shape, dt))

        win = [sb(f"win{i}", [P, KD, 2 * DI]) for i in range(2)]
        wx = [sb(f"wx{i}", [P, J, XR]) for i in range(2)]
        wdt2 = sb("wdt2", [R_DT[0] + RANK, DI])
        wdt = [wdt2[r:r + RANK, :] for r in R_DT]
        wout = [sb(f"wout{i}", [P, J, D]) for i in range(2)]
        convw = [sb(f"convw{i}", [P, J, NTAP]) for i in range(2)]
        vecs = [sb(f"vecs{i}", [P, 3, J]) for i in range(2)]
        aneg = [sb(f"aneg{i}", [P, J, NS]) for i in range(2)]
        norm = sb("norm", [P, 2, KD])
        wexp = sb("wexp", [P, NE * HD // P, D])
        simn = sb("simn", [P, KD, NE])
        sgate = sb("sgate", [P, NE])
        rank = sb("rank", [P, NE])
        ident = sb("ident", [P, P])
        causal = sb("causal", [P, P])
        mhalf = sb("mhalf", [P, NE])
        zero3 = sb("zero3", [P, NTAP - 1])
        one = sb("one", [P, 1])
        pick = sb("pick", [XR, NS], BF16)
        part = sb("part", [XR, 2])
        decay = sb("decay", [P, RING, UL])
        binp = sb("binp", [P, RING, UL])
        hst = sb("hst", [P, 2, J, UL])
        acc = sb("acc", [P, 2, UT, DI])
        bbc = sb("bbc", [P, 2, UL])
        carry = sb("carry", [P, J, NS])
        upad = sb("upad", [P, 2, UL + NTAP - 1])
        halo = sb("halo", [P, J, NTAP - 1])
        diag = sb("diag", [P, NTAP, P])
        us = sb("us", [P, J, UL])
        dtb = sb("dtb", [P, 2, J, UL])
        dub = sb("dub", [P, 2, J, UL])
        xd = sb("xd", [XR, UL])
        bparts = sb("bparts", [XR, 2, UL], BF16)
        ct = sb("ct", [P, 2, UT, NS])
        sz = sb("sz", [P, J, UL])
        yg = sb("yg", [P, 2, J, P])
        ytmp = sb("ytmp", [P, D])
        hyt = sb("hyt", [P, 2, D])
        ga_bc = sb("ga_bc", [P, D])
        xnT = sb("xnT", [P, KD, L])
        bufx = sb("bufx", [P, NT, D])
        bufh = sb("bufh", [P, NT, D])
        x2f = sb("x2f", [P, NT, D])
        h2T = sb("h2T", [P, KD, L])
        modp = sb("modp", [P, 3, D])
        modl = sb("modl", [P, 2, D])
        gb_bc = sb("gb_bc", [P, D])
        stx = sb("stx", [P, NT, 6])
        mvx = sb("mvx", [P, NT, 2])
        mvh = sb("mvh", [P, NT, 2])
        mvl = sb("mvl", [P, NT, 2])
        rsx = sb("rsx", [P, 4, NT])
        ve = sb("ve", [P, 4, NT])
        rw = sb("rw", [P, NT, NE])
        attn = sb("attn", [P, HD])
        small = sb("small", [P, 4, NT])
        mxs = sb("mxs", [P, 4])
        rsum = sb("rsum", [P, 2])
        ft = sb("ft", [P, 2, D])

        basetmp = ft[:]
        qkvb = bufh[:].rearrange("p a b -> p (a b)")[:, 0:NT * QW].rearrange("p (t c) -> p t c", t=NT)
        xflat = bufx[:].rearrange("p a b -> p (a b)")
        prob, probT = xflat[:, 0:L], xflat[:, L:2 * L].rearrange("p (k t) -> p k t", k=NT)
        mixed = qkvb[:, :, 0:2 * HD]
        qkT = h2T
        xnt = h2T[:].rearrange("p k t -> p (k t)").rearrange("p (t c) -> p t c", t=NT)
        wo = wexp
        wq = wexp[:].rearrange("p a b -> p (a b)")[:, 0:2 * KD * EC * QW].rearrange("p (a k n) -> p a k n", a=2, k=KD)
        gt = [xflat[:, P * i:P * (i + 1)].rearrange("p (t e) -> p t e", t=NT) for i in range(6)]
        junk = xflat[:, L:2 * L].bitcast(BF16).rearrange("p (t c) -> p t c", t=NT)
        cT = us[:, 0, 0:KD * B].rearrange("p (k b) -> p k b", k=KD)
        wmod = hst[:].rearrange("p a j t -> p (a j t)")[:, 0:KD * 6 * D].rearrange("p (k n) -> p k n", k=KD)
        mods = x2f[:].rearrange("p a b -> p (a b)")[0:B, 0:6 * D].rearrange("p (m c) -> p m c", m=6)
        simraw = us[:, 1, 0:KD * NE].rearrange("p (k e) -> p k e", k=KD)
        simsq = us[:, 2, 0:KD * NE].rearrange("p (k e) -> p k e", k=KD)
        simrn = us[:, 3, 0:NE]
        ones = sz[:, 0, 0:P]
        pickf = sz[0:XR, 3, 0:NS]

        def b_split(s):
            two = dtb[0:XR, s % 2, 2, :].bitcast(BF16)
            return two[:, 0:UL], two[:, UL:2 * UL], dtb[0:XR, s % 2, 3, :]
        gsgn = [sz[0:B, 1, 0:D], sz[0:B, 2, 0:D]]

        hT = [ctx.enter_context(nc.psum_tensor(f"hT{i}", [P, 512], F32)) for i in range(UT)]
        bps = ctx.enter_context(nc.psum_tensor("bps", [P, 512], F32))
        side = [ctx.enter_context(nc.psum_tensor(f"side{i}", [P, 512], F32)) for i in range(SIDE)]

        sems = {}

        def sem(name):
            if name not in sems:
                sems[name] = ctx.enter_context(nc.semaphore(name))
            return sems[name]

        s_w, s_mods, s_modst = sem("weights_in"), sem("mods_ready"), sem("mods_stored")
        s_x, s_modp, s_modl = sem("x_in"), sem("modp_in"), sem("modl_in")
        s_ga, s_gb, s_base = sem("ga_in"), sem("gb_in"), sem("base_stored")
        s_hyl = [sem("partial_in0"), sem("partial_in1")]
        s_hys = [sem("partial_stored0"), sem("partial_stored1")]
        s_wq = [sem("wq_in0"), sem("wq_in1")]
        s_wo = sem("wo_in")
        s_out = [sem("out_stored0"), sem("out_stored1")]
        s_bp, s_bc, s_dec, s_in = sem("b_spread"), sem("b_copied"), sem("decay_ready"), sem("input_ready")
        s_scan, s_turn, s_acc, s_car = sem("scanned"), sem("state_turned"), sem("readout_added"), sem("carried")
        pe_ = {st: sem(f"pe_{st}") for st in PER}
        tk_ = {st: sem(f"took_{st}") for st in PER}
        s_stx, s_aggx, s_pwv, s_pw, s_pn = sem("stx"), sem("aggx"), sem("pw_var"), sem("pw"), sem("normed_x")
        s_ph1, s_ph, s_sth, s_aggh = sem("scaled_x"), sem("mod_x"), sem("sth"), sem("aggh")
        s_pw2v, s_pw2, s_pb1, s_pb, s_pxn = sem("pw2_var"), sem("pw2"), sem("gated_h"), sem("base"), sem("normed_h")
        s_dg, s_sl, s_sp0, s_sp1, s_ad, s_dm = (sem("diag"), sem("silu_u"), sem("softplus_exp"), sem("softplus_ln"),
                                                sem("dt"), sem("dtu"))
        s_pk = sem("pick_row")
        s_brest, s_bmid, s_bparts = sem("b_rest"), sem("b_mid"), sem("b_parts")
        s_zs, s_yadd = sem("silu_z"), sem("unit_out")
        s_stl, s_aggl, s_pw3v, s_pw3, s_ln = sem("stl"), sem("aggl"), sem("pw3_var"), sem("pw3"), sem("normed_2")
        s_lh1, s_lh, s_sq, s_rn1, s_rn = sem("scaled_2"), sem("mod_2"), sem("squares"), sem("rn_pow"), sem("rn")
        s_gate, s_gexp, s_gate2 = sem("gate_step"), sem("gate_exp"), sem("gate_norm")
        s_qst, s_s, s_exp, s_ri, s_mix, s_fadd = (sem("expert_added"), sem("score_step"), sem("prob"), sem("rsum_inv"),
                                                  sem("mixed"), sem("final"))
        s_c, s_pc, s_ac, s_vc, s_pec = (sem("consts"), sem("pool_once"), sem("act_once"), sem("dve_once"),
                                        sem("pe_once"))
        NGATE = 22
        tk_["l_lg"] = s_gate

        def wait_apart(eng, *waits):
            waits = [(sm, v if isinstance(v, int) else eng.compute_val(v)) for sm, v in waits]
            eng.wait_ge(s_c, 1)
            for sm, v in waits:
                need(eng, sm, v)

        def holder(tenant, b):
            if tenant is None:
                return s_c, 1
            if tenant == "scan":
                return s_acc, B * 4 * STEPS
            st, db, s, k = tenant
            if st in ("U", "V", "W", "D", "Z", "yT", "yo"):
                k = 4 * s + k
            elif st in ("X", "C"):
                k = s
            if st == "q":
                return s_qst, done(b + db, 4 * PER[st], 4 * k + 3)
            per = NGATE if st == "l_lg" else PER[st]
            return tk_[st], done(b + db, per, k)

        PLAN = plan()
        WEIGHTS = []

        def walk(eng, stages, core, flush):
            def pieces(row, b, seg):
                for (st, db, s, k), got in row:
                    if st in stages:
                        stages[st](b + db, s, k, [(side + hT)[i] for i, _ in got], [(t, b) for _, t in got], seg)

            def body(b, seg):
                for i, row in enumerate(PLAN[seg]):
                    core(b, i // NS, i % NS, seg)
                    pieces(row, b, seg)

            pieces(PLAN["prologue"][0], -1, "prologue")
            core(-1, NU - 1, NS, "prologue")
            body(0, "first")
            with eng.Fori(1, B - 1) as b:
                body(b, "steady")
            body(B - 1, "last")
            flush()
            pieces(PLAN["epilogue"][0], B, "epilogue")

        block = ctx.enter_context(nc.Block())

        @block.sync
        def _(sp):
            n = 0
            pairs = []
            for i, d in enumerate("fb"):
                pairs += [(win[i][:], a[f"win_{d}"]), (wdt[i], a[f"wdt_{d}"]), (wout[i][:], a[f"wout_{d}"]),
                          (convw[i][:], a[f"convw_{d}"]), (vecs[i][:], a[f"vecs_{d}"]),
                          (aneg[i][:], a[f"alog_{d}"])]
            pairs += [(norm[:], a["norm"]), (simraw, a["sim"]), (cT, a["cT"]), (wmod, a["wmod"]),
                      (sgate[:], a["gates"].partition_broadcast(P)), (rank[:], a["rank"].partition_broadcast(P))]
            for dst, src in pairs:
                sp.dma_start(dst, src).then_inc(s_w, 16)
                n += 16
            for i, d in enumerate("fb"):
                for r, what in enumerate(ROWS_OF[i]):
                    c = {"dt": 0, "B": RANK, "C": RANK + NS}[what]
                    sp.dma_start(wx[i][:, :, NS * r:NS * (r + 1)], a[f"wx_{d}"][:, :, c:c + NS]).then_inc(s_w, 16)
                    n += 16
            WEIGHTS.append(n)
            sp.wait_ge(s_mods, 1)
            sp.dma_start(mod_d, mods).then_inc(s_modst, 16)
            sp.wait_ge(s_modst, 16)

            def row(b, m0, m1):
                return mod_d[bass.ds(b, 1), m0:m1, :].partition_broadcast(P).rearrange("p a m c -> p (a m) c")

            def tokens(t, b):
                return t[bass.ds(b, 1), :, :].rearrange("a (t p) c -> p (a t) c", p=P)

            def token_tile(t, b, k):
                return t[bass.ds(b, 1), k * P:(k + 1) * P, :].rearrange("a p c -> p (a c)")

            def x_ld(b, s, k, *_):
                need(sp, pe_["FO"], done(b - 2, PER["FO"], NT - 1))
                need(sp, s_base, (b) * 16)
                sp.dma_start(bufx[:], tokens(a["x"], b)).then_inc(s_x, 16)
                need(sp, s_pb, done(b - 1, 4, 3))
                sp.dma_start(modp[:], row(b, 0, 3)).then_inc(s_modp, 16)

            def p_base(b, s, k, *_):
                if k == 3:
                    need(sp, s_pb, done(b, 4, 3))
                    sp.dma_start(tokens(hy_d, b), bufx[:]).then_inc(s_base, 16)

            def g_ld(b, s, k, *_):
                need(sp, tk_["yo"], done(b - 1, PER["yo"], 15))
                sp.dma_start(ga_bc[:], row(b, 2, 3).rearrange("p m c -> p (m c)")).then_inc(s_ga, 16)

            def bl(b, s, k, *_):
                back, half, _0 = unit(s)
                waits = [(s_yadd, done(b, 16, 4 * s + k - 2))]
                if back:
                    waits += [(x, 16 * done(b, 4, 3)) for x in s_hys]
                else:
                    waits += [(s_base, (b + 1) * 16), (s_hys[k % 2], 16 * done(b, 4, 2 * s + k // 2 - 1))]
                wait_apart(sp, *waits)
                sp.dma_start(hyt[:, k % 2, :], token_tile(hy_d, b, tile_of(s, k))).then_inc(s_hyl[k % 2], 16)

            def yo(b, s, k, *_):
                if not unit(s)[0]:
                    need(sp, s_yadd, done(b, 16, 4 * s + k))
                    sp.dma_start(token_tile(hy_d, b, tile_of(s, k)), hyt[:, k % 2, :]).then_inc(s_hys[k % 2], 16)

            def l_ld(b, s, k, *_):
                sp.dma_start(modl[:], row(b, 3, 5)).then_inc(s_modl, 16)
                sp.dma_start(gb_bc[:], row(b, 5, 6).rearrange("p m c -> p (m c)")).then_inc(s_gb, 16)

            def w_ld(b, s, g, *_):
                if g >= 2:
                    need(sp, pe_["q"], done(b, 32, 4 * (g - 2) + 3))
                sp.dma_start(wq[:, g % 2], a["wqkv"][g]).then_inc(s_wq[g % 2], 16)

            def a_T(b, s, k, *_):
                if k == 0:
                    need(sp, pe_["q"], done(b, 32, 31))
                    sp.dma_start(wo[:], a["wo"]).then_inc(s_wo, 16)

            def FO(b, s, k, *_):
                need(sp, s_fadd, done(b, 8, k))
                sp.dma_start(token_tile(out, b, k), ft[:, k % 2, :]).then_inc(s_out[k % 2], 16)

            walk(sp, {"x_ld": x_ld, "p_base": p_base, "g_ld": g_ld, "bl": bl, "yo": yo, "l_ld": l_ld,
                      "w_ld": w_ld, "a_T": a_T, "FO": FO}, lambda *_: None, lambda: None)
            for q in range(2):
                sp.wait_ge(s_out[q], 16 * B * NT // 2)
                sp.wait_ge(s_hys[q], 16 * B * 4)

        @block.tensor
        def _(pe):
            def take(tenants):
                for t, b in tenants:
                    need(pe, *holder(t, b))

            pe.wait_ge(s_w, WEIGHTS[0])
            pe.wait_ge(s_c, 1)
            pe.wait_ge(s_ac, 2)
            for m in range(3):
                for k in range(KD):
                    mm = pe.matmul(hT[m][0:B, :], cT[:, k, :], wmod[:, k, 512 * m:512 * (m + 1)],
                                   start=(k == 0), stop=(k == KD - 1))
            for k in range(KD):
                mm = pe.matmul(hT[3][:, 0:NE], ones, simsq[:, k, :], start=(k == 0), stop=(k == KD - 1))
            mm.then_inc(s_pec, 1)

            def p_T(b, s, i, bk, tn, seg):
                take(tn)
                need(pe, s_pxn, done(b, 2, i // 2))
                for k in range(KD):
                    for q in range(2):
                        mm = pe.transpose(bk[0][:, 256 * k + P * q:256 * k + P * (q + 1)],
                                          xnt[:, 2 * i + q, k * P:(k + 1) * P], ident[:])
                mm.then_inc(pe_["p_T"], 1)

            def U(b, s, j, bk, tn, seg):
                back, half, lo = unit(s)
                take(tn)
                need(pe, tk_["p_T"], done(b, 4, 3))
                for k in range(KD):
                    x = xnT[:, k, lo:lo + UL]
                    mm = pe.matmul(bk[0][:], win[back][:, k, j * P:(j + 1) * P], x[:, ::-1] if back else x,
                                   start=(k == 0), stop=(k == KD - 1))
                mm.then_inc(pe_["U"], 1)

            def V(b, s, j, bk, tn, seg):
                take(tn)
                need(pe, tk_["U"], done(b, 16, 4 * s + j))
                need(pe, s_dg, done(b, 20, 5 * s + j))
                for k in range(NTAP):
                    mm = pe.matmul(bk[0][:], diag[:, k, :], upad[:, j % 2, k:k + UL], start=(k == 0),
                                   stop=(k == NTAP - 1))
                mm.then_inc(pe_["V"], 1)

            def W(b, s, j, bk, tn, seg):
                take(tn)
                need(pe, s_sl, done(b, 4, s))
                need(pe, s_dg, done(b, 20, 5 * s + 4))
                for t in range(UT):
                    mm = pe.matmul(bk[0][:, t * P:(t + 1) * P], us[:, j, t * P:(t + 1) * P], diag[:, j, :],
                                   start=True, stop=True)
                mm.then_inc(pe_["W"], 1)

            def X(b, s, _k, bk, tn, seg):
                take(tn)
                need(pe, s_sl, done(b, 4, s))
                for j in range(J):
                    mm = pe.matmul(bk[0][0:XR, :], wx[s // 2][:, j, :], us[:, j, :], start=(j == 0), stop=(j == J - 1))
                mm.then_inc(pe_["X"], 1)

            def C(b, s, _k, bk, tn, seg):
                wait_apart(pe, holder(*tn[0]), (tk_["X"], done(b, 4, s)))
                r = R_C[s // 2]
                for t in range(UT):
                    mm = pe.transpose(bk[0][:, t * NS:(t + 1) * NS], xd[r:r + NS, t * P:(t + 1) * P],
                                      ident[r:r + NS, r:r + NS])
                mm.then_inc(pe_["C"], 1)

            def Dt(b, s, j, bk, tn, seg):
                take(tn)
                need(pe, tk_["X"], done(b, 4, s))
                r = R_DT[s // 2]
                pe.matmul(bk[0][:], wdt[s // 2][:, j * P:(j + 1) * P], xd[r:r + RANK, :],
                          start=True, stop=True).then_inc(pe_["D"], 1)

            def Z(b, s, j, bk, tn, seg):
                back, half, lo = unit(s)
                take(tn)
                need(pe, tk_["p_T"], done(b, 4, 3))
                for k in range(KD):
                    mm = pe.matmul(bk[0][:], win[back][:, k, DI + j * P:DI + (j + 1) * P], xnT[:, k, lo:lo + UL],
                                   start=(k == 0), stop=(k == KD - 1))
                mm.then_inc(pe_["Z"], 1)

            def yT(b, s, k, bk, tn, seg):
                take(tn)
                need(pe, s_acc, done(b, 4 * STEPS, 4 * NS * s + 4 * NS - 1))
                for j in range(J):
                    mm = pe.transpose(bk[0][:, j * P:(j + 1) * P], acc[:, s % 2, k, j * P:(j + 1) * P], ident[:])
                mm.then_inc(pe_["yT"], 1)

            def yo(b, s, k, bk, tn, seg):
                take(tn)
                need(pe, tk_["yT"], done(b, 16, 4 * s + k))
                for j in range(J):
                    mm = pe.matmul(bk[0][:, 0:D], yg[:, k % 2, j, :], wout[s // 2][:, j, :], start=(j == 0),
                                   stop=(j == J - 1))
                mm.then_inc(pe_["yo"], 1)

            def l_T(b, s, i, bk, tn, seg):
                take(tn)
                need(pe, s_lh, done(b, 4, i))
                for k in range(KD):
                    for q in range(2):
                        mm = pe.transpose(bk[0][:, 256 * k + P * q:256 * k + P * (q + 1)],
                                          bufh[:, 2 * i + q, k * P:(k + 1) * P], ident[:])
                mm.then_inc(pe_["l_T"], 1)

            def l_lg(b, s, _k, bk, tn, seg):
                take(tn)
                need(pe, tk_["l_T"], done(b, 4, 3))
                for t in range(NT):
                    for k in range(KD):
                        mm = pe.matmul(bk[0][:, t * NE:(t + 1) * NE], h2T[:, k, t * P:(t + 1) * P], simn[:, k, :],
                                       start=(k == 0), stop=(k == KD - 1))
                mm.then_inc(pe_["l_lg"], 1)

            def q(b, s, i, bk, tn, seg):
                g, pair = i // 4, i % 4
                take(tn)
                need(pe, s_wq[g % 2], 16 * done(b, 4, g // 2))
                for h in range(2):
                    t = 2 * pair + h
                    for k in range(KD):
                        mm = pe.matmul(bk[h][:, 0:EC * QW], h2T[:, k, t * P:(t + 1) * P], wq[:, g % 2, k, :],
                                       start=(k == 0), stop=(k == KD - 1))
                mm.then_inc(pe_["q"], 1)

            def a_T(b, s, i, bk, tn, seg):
                wait_apart(pe, holder(*tn[0]), (s_qst, done(b, 128, 127)))
                for w in range(2):
                    for h in range(2):
                        mm = pe.transpose(bk[0][0:HD, 256 * w + P * h:256 * w + P * (h + 1)],
                                          qkvb[:, 2 * i + h, w * HD:(w + 1) * HD], ident[:])
                mm.then_inc(pe_["a_T"], 1)

            def S(b, s, i, bk, tn, seg):
                take(tn)
                need(pe, tk_["a_T"], done(b, 4, 3))
                for h in range(len(bk)):
                    w = min((i + 1) * P - 512 * h, 512)
                    mm = pe.matmul(bk[h][:, 0:w], qkT[0:HD, 0, i * P:(i + 1) * P], qkT[0:HD, 1, 512 * h:512 * h + w],
                                   start=True, stop=True)
                mm.then_inc(pe_["S"], 1)

            def PT(b, s, i, bk, tn, seg):
                take(tn)
                need(pe, s_exp, done(b, 8, i))
                for k in range(i + 1):
                    mm = pe.transpose(bk[k // 4][:, (k % 4) * P:(k % 4 + 1) * P], prob[:, k * P:(k + 1) * P], ident[:])
                mm.then_inc(pe_["PT"], 1)

            def PV(b, s, i, bk, tn, seg):
                take(tn)
                need(pe, tk_["PT"], done(b, 8, i))
                for k in range(i + 1):
                    mm = pe.matmul(bk[0][:, 0:HD], probT[:, k, :], qkvb[:, k, 2 * HD:3 * HD], start=(k == 0),
                                   stop=(k == i))
                mm.then_inc(pe_["PV"], 1)

            def OT(b, s, i, bk, tn, seg):
                take(tn)
                need(pe, s_mix, done(b, 8, i))
                for k in range(NT):
                    mm = pe.transpose(bk[k // 4][:, (k % 4) * P:(k % 4 + 1) * P], mixed[:, k, :], ident[:])
                mm.then_inc(pe_["OT"], 1)

            def FO(b, s, i, bk, tn, seg):
                take(tn)
                need(pe, tk_["OT"], done(b, 8, i))
                need(pe, s_wo, 16 * (b + 1))
                for k in range(NT):
                    mm = pe.matmul(bk[0][:, 0:D], probT[:, k, :], wo[:, k, :], start=(k == 0), stop=(k == NT - 1))
                mm.then_inc(pe_["FO"], 1)

            def turn(b, i):
                need(pe, s_scan, done(b, 4 * STEPS, 4 * i + 3))
                for t in range(UT):
                    need(pe, s_acc, done(b, 4 * STEPS, 4 * (i - 1) + t))
                    for j in range(J):
                        mm = pe.transpose(hT[t][:, j * P:(j + 1) * P], hst[:, i % 2, j, t * P:(t + 1) * P], ident[:])
                    mm.then_inc(s_turn, 1)

            def core(b, s, n, seg):
                i = NS * s + n
                nxt = i + 1 if seg != "prologue" else i
                if not (seg == "last" and nxt == STEPS):
                    m = nxt % NS
                    need(pe, s_bparts, done(b, 4, nxt // NS))
                    need(pe, s_bc, done(b, STEPS, nxt - 1))
                    pe.matmul(bps[:], pick[:, m:m + 1].to_broadcast([XR, P]), bparts[:, (nxt // NS) % 2, :],
                              start=True, stop=True).then_inc(s_bp, 1)
                if seg != "prologue" and not (seg == "first" and i == 0):
                    turn(b, i - 1)

            pe.wait_ge(s_vc, 9)
            pe.wait_ge(s_ac, 3)
            walk(pe, {"p_T": p_T, "U": U, "V": V, "W": W, "X": X, "C": C, "D": Dt, "Z": Z, "yT": yT, "yo": yo,
                      "l_T": l_T, "l_lg": l_lg, "q": q, "a_T": a_T, "S": S, "PT": PT, "PV": PV, "OT": OT, "FO": FO},
                 core, lambda: turn(B - 1, STEPS - 1))

        @block.scalar
        def _(act):
            act.wait_ge(s_w, WEIGHTS[0])
            act.wait_ge(s_pc, 2)
            act.activation(cT, cT, ACT.Silu).then_inc(s_ac, 1)
            act.activation(simsq, simraw, ACT.Square).then_inc(s_ac, 1)
            act.activation(sgate[:], sgate[:], ACT.Sigmoid)
            for i in range(2):
                ins = act.activation(aneg[i][:], aneg[i][:], ACT.Exp)
            ins.then_inc(s_ac, 1)

            def p_T(b, s, i, bk, tn, seg):
                act.wait_ge(pe_["p_T"], done(b, 4, i))
                for k in range(KD):
                    ins = act.activation(xnT[:, k, 256 * i:256 * (i + 1)], bk[0][:, 256 * k:256 * (k + 1)], ACT.Identity,
                                         bias=norm[:, 1, k:k + 1], scale=norm[:, 0, k:k + 1])
                ins.then_inc(tk_["p_T"], 1)

            def U(b, s, j, bk, tn, seg):
                half = s % 2
                act.wait_ge(pe_["U"], done(b, 16, 4 * s + j))
                act.activation(upad[:, j % 2, 0:NTAP - 1], halo[:, j, :] if half else zero3[:], ACT.Copy)
                if not half:
                    act.activation(halo[:, j, :], bk[0][:, UL - NTAP + 1:UL], ACT.Copy)
                act.activation(upad[:, j % 2, NTAP - 1:], bk[0][:], ACT.Copy).then_inc(tk_["U"], 1)

            def V(b, s, j, bk, tn, seg):
                act.wait_ge(pe_["V"], done(b, 16, 4 * s + j))
                need(act, s_dm, done(b, 16, 4 * s - 1))
                act.activation(us[:, j, :], bk[0][:], ACT.Identity, bias=vecs[s // 2][:, 0, j:j + 1])\
                   .then_inc(tk_["V"], 1)

            def sl(b, s, k, bk, tn, seg):
                act.wait_ge(tk_["V"], done(b, 16, 4 * s + 3))
                act.activation(us[:], us[:], ACT.Silu).then_inc(s_sl, 1)

            def W(b, s, j, bk, tn, seg):
                act.wait_ge(pe_["W"], done(b, 16, 4 * s + j))
                need(act, pe_["yT"], done(b, 16, 4 * s - 5))
                act.activation(acc[:, s % 2, :, j * P:(j + 1) * P], bk[0][:].rearrange("p (t d) -> p t d", t=UT),
                               ACT.Copy).then_inc(tk_["W"], 1)

            def X(b, s, k, bk, tn, seg):
                act.wait_ge(pe_["X"], done(b, 4, s))
                need(act, s_in, done(b, 4 * STEPS, 4 * NS * (s - 1) - 1))
                need(act, s_bparts, done(b, 4, s - 1))
                act.activation(b_split(s)[0], bk[0][0:XR, :], ACT.Copy)
                act.activation(xd[:], bk[0][0:XR, :], ACT.Copy).then_inc(tk_["X"], 1)

            def Xm(b, s, k, bk, tn, seg):
                act.wait_ge(s_brest, done(b, 4, s))
                act.activation(b_split(s)[1], b_split(s)[2], ACT.Copy).then_inc(s_bmid, 1)

            def C(b, s, k, bk, tn, seg):
                act.wait_ge(pe_["C"], done(b, 4, s))
                need(act, s_acc, done(b, 4 * STEPS, 4 * NS * (s - 1) - 1))
                act.activation(ct[:, s % 2].rearrange("p t n -> p (t n)"), bk[0][:, 0:UT * NS], ACT.Copy)\
                   .then_inc(tk_["C"], 1)

            def Dt(b, s, j, bk, tn, seg):
                bias = vecs[s // 2][:, 1, j:j + 1]
                act.wait_ge(pe_["D"], done(b, 16, 4 * s + j))
                if j == 0:
                    need(act, s_bparts, done(b, 4, s))
                need(act, s_in, done(b, 4 * STEPS, 4 * NS * (s - 1) - 1))
                act.activation(dtb[:, s % 2, j, :], bk[0][:], ACT.Abs, bias=bias)
                act.activation(dub[:, s % 2, j, :], bk[0][:], ACT.Relu, bias=bias).then_inc(tk_["D"], 1)

            def sp_(b, s, k, bk, tn, seg):
                v = dtb[:, s % 2]
                act.wait_ge(tk_["D"], done(b, 16, 4 * s + 3))
                act.activation(v, v, ACT.Exp, scale=-1.0).then_inc(s_sp0, 1)
                act.wait_ge(s_sp0, done(b, 4, s))
                act.activation(v, v, ACT.Ln, bias=one[:, 0:1]).then_inc(s_sp1, 1)

            def Z(b, s, j, bk, tn, seg):
                act.wait_ge(pe_["Z"], done(b, 16, 4 * s + j))
                need(act, tk_["yT"], done(b, 16, 4 * s - 1))
                act.activation(sz[:, j, :], bk[0][:], ACT.Copy).then_inc(tk_["Z"], 1)

            def zs(b, s, k, bk, tn, seg):
                act.wait_ge(tk_["Z"], done(b, 16, 4 * s + 3))
                act.activation(sz[:], sz[:], ACT.Silu).then_inc(s_zs, 1)

            def l_T(b, s, i, bk, tn, seg):
                act.wait_ge(pe_["l_T"], done(b, 4, i))
                act.activation(h2T[:, :, 256 * i:256 * (i + 1)], bk[0][:].rearrange("p (k t) -> p k t", k=KD),
                               ACT.Copy).then_inc(tk_["l_T"], 1)

            def l_sq(b, s, k, bk, tn, seg):
                act.wait_ge(s_lh, done(b, 4, 3))
                act.wait_ge(s_base, 16 * (b + 2) if seg != "epilogue" else 16 * B)
                for t in range(NT):
                    ins = act.activation(junk[:, t, :], bufh[:, t, :], ACT.Square, accum_out=ve[:, 3, t:t + 1])
                ins.then_inc(s_sq, 1)

            def l_ge(b, s, k, bk, tn, seg):
                act.wait_ge(s_gate, done(b, NGATE, NGATE - 1))
                act.activation(gt[0], gt[0], ACT.Exp).then_inc(s_gexp, 1)

            def a_T(b, s, i, bk, tn, seg):
                act.wait_ge(pe_["a_T"], done(b, 4, i))
                act.activation(qkT[0:HD, :, 256 * i:256 * (i + 1)], bk[0][0:HD, :].rearrange("p (k t) -> p k t", k=2),
                               ACT.Copy).then_inc(tk_["a_T"], 1)

            def E(b, s, i, bk, tn, seg):
                act.wait_ge(tk_["S"], done(b, 8, i))
                if i:
                    act.wait_ge(s_ri, done(b, 8, i - 1))
                v = prob[:, 0:(i + 1) * P]
                act.activation(v, v, ACT.Exp, bias=mxs[:, 3:4], scale=HD ** -0.5, accum_out=rsum[:, 0:1])\
                   .then_inc(s_exp, 1)

            def PT(b, s, i, bk, tn, seg):
                act.wait_ge(pe_["PT"], done(b, 8, i))
                for h in range(len(bk)):
                    w = min(i + 1 - 4 * h, 4)
                    ins = act.activation(probT[:, 4 * h:4 * h + w, :],
                                         bk[h][:, 0:w * P].rearrange("p (k t) -> p k t", k=w), ACT.Copy)
                ins.then_inc(tk_["PT"], 1)

            def OT(b, s, i, bk, tn, seg):
                act.wait_ge(pe_["OT"], done(b, 8, i))
                for h in range(2):
                    ins = act.activation(probT[:, 4 * h:4 * h + 4, :], bk[h][:].rearrange("p (k t) -> p k t", k=4),
                                         ACT.Copy)
                ins.then_inc(tk_["OT"], 1)

            def core(b, s, n, seg):
                i = NS * s + n
                nxt = i + 1 if seg != "prologue" else i
                if seg != "prologue":
                    if n == 0:
                        act.wait_ge(s_ad, done(b, 16, 4 * s + 3))
                    for j in range(J):
                        r = 4 * i + j
                        need(act, s_scan, done(b, 4 * STEPS, r - RING))
                        act.activation(decay[:, r % RING, :], dtb[:, s % 2, j, :], ACT.Exp,
                                       scale=aneg[s // 2][:, j, n:n + 1]).then_inc(s_dec, 1)
                if not (seg == "last" and nxt == STEPS):
                    act.wait_ge(s_bp, done(b, STEPS, nxt))
                    need(act, s_in, done(b, 4 * STEPS, 4 * (nxt - 2) + 3))
                    act.activation(bbc[:, nxt % 2, :], bps[:], ACT.Copy).then_inc(s_bc, 1)

            walk(act, {"p_T": p_T, "U": U, "V": V, "sl": sl, "W": W, "X": X, "Xm": Xm, "C": C, "D": Dt, "sp": sp_, "Z": Z,
                       "zs": zs, "l_T": l_T, "l_sq": l_sq, "l_ge": l_ge, "a_T": a_T, "E": E, "PT": PT, "OT": OT},
                 core, lambda: None)

        @block.gpsimd
        def _(pool):
            pool.memset(pickf, 0.0)
            pool.memset(part[:], -1.0).then_inc(s_pc, 1)
            pool.memset(ident[:], 0.0)
            pool.memset(causal[:], 0.0)
            pool.memset(zero3[:], 0.0)
            pool.memset(ones, 1.0)
            pool.memset(mhalf[:], -0.5)
            pool.memset(one[:], 1.0).then_inc(s_pc, 1)
            pool.wait_ge(s_pc, 2)
            pool.affine_select(out=ident[:], in_=ident[:], compare_op=ALU.not_equal, fill=1.0, base=0,
                               pattern=[[-1, P]], channel_multiplier=1)
            for i, r in enumerate(R_B):
                pool.affine_select(out=pickf, in_=pickf, compare_op=ALU.not_equal, fill=1.0, base=-r,
                                   pattern=[[-1, NS]], channel_multiplier=1).then_inc(s_pk, 1)
                pool.wait_ge(s_pk, i + 1)
            for q in range(2):
                pool.affine_select(out=part[:, q:q + 1], in_=part[:, q:q + 1], compare_op=ALU.is_ge, fill=0.0,
                                   base=-R_B[q + 1], pattern=[[0, 1]], channel_multiplier=1)
            pool.tensor_copy(pick[:], pickf)
            pool.affine_select(out=causal[:], in_=causal[:], compare_op=ALU.is_ge, fill=-BIG, base=0,
                               pattern=[[-1, P]], channel_multiplier=1).then_inc(s_c, 1)
            pool.wait_ge(s_ac, 3)
            for i in range(2):
                ins = pool.tensor_scalar(aneg[i][:], aneg[i][:], -1.0, None, ALU.mult)
            ins.then_inc(s_pc, 1)
            pool.wait_ge(s_vc, 1)
            pool.tensor_tensor(simrn, simrn, mhalf[:], ALU.pow).then_inc(s_pc, 1)
            pool.wait_ge(s_pc, 4)
            pool.tensor_scalar(simrn, simrn, 1e12, None, ALU.min).then_inc(s_pc, 1)
            pool.wait_ge(s_pc, 5)
            pool.tensor_tensor(simn[:], simraw, simrn.unsqueeze(1).broadcast_to([P, KD, NE]), ALU.mult)\
                .then_inc(s_pc, 1)
            pool.wait_ge(s_vc, 9)

            def power(mv, w, b, s_in_, s_mid, s_end, parts=1, i=0):
                t0, t1 = NT // parts * i, NT // parts * (i + 1)
                wait_apart(pool, (s_in_, done(b, parts, i)))
                pool.tensor_scalar(ve[:, w, t0:t1], mv[:, t0:t1, 1], EPS, None, ALU.add).then_inc(s_mid, 1)
                pool.wait_ge(s_mid, done(b, parts, i))
                pool.tensor_tensor(rsx[:, w, t0:t1], ve[:, w, t0:t1], mhalf[:, 0:t1 - t0], ALU.pow).then_inc(s_end, 1)

            def p_pw(b, *_):
                power(mvx, 0, b, s_aggx, s_pwv, s_pw)

            def p_pw2(b, s, i, *_):
                power(mvh, 1, b, s_aggh, s_pw2v, s_pw2, 2, i)

            def l_pw(b, *_):
                power(mvl, 2, b, s_aggl, s_pw3v, s_pw3)

            def modulate(b, i, mod, s_mid, s_end):
                v = bufh[:, 2 * i:2 * i + 2, :]
                pool.tensor_tensor(v, v, mod[:, 1:2, :].broadcast_to([P, 2, D]), ALU.mult).then_inc(s_mid, 1)
                pool.wait_ge(s_mid, done(b, 4, i))
                pool.tensor_tensor(v, v, mod[:, 0:1, :].broadcast_to([P, 2, D]), ALU.add).then_inc(s_end, 1)

            def p_h(b, s, i, *_):
                pool.wait_ge(s_pn, done(b, 2, i // 2))
                pool.wait_ge(s_modp, 16 * (b + 1))
                modulate(b, i, modp, s_ph1, s_ph)

            def p_base(b, s, i, *_):
                v = bufx[:, 2 * i:2 * i + 2, :]
                if i == 0:
                    for q in range(2):
                        need(pool, s_out[q], 16 * done(b - 2, 4, 3))
                else:
                    pool.wait_ge(s_pb, done(b, 4, i - 1))
                pool.tensor_tensor(basetmp, bufh[:, 2 * i:2 * i + 2, :], modp[:, 2:3, :].broadcast_to([P, 2, D]),
                                   ALU.mult).then_inc(s_pb1, 1)
                pool.wait_ge(s_pb1, done(b, 4, i))
                pool.tensor_tensor(v, v, basetmp, ALU.add).then_inc(s_pb, 1)

            def dg(b, s, j, *_):
                back = s // 2
                if j == 0:
                    need(pool, tk_["W"], done(b, 16, 4 * s - 1))
                else:
                    need(pool, tk_["V"], done(b, 16, 4 * s + j - 1))
                w = convw[back][:, j, :] if j < J else vecs[back][:, 2, :]
                pool.tensor_tensor(diag[:], ident[:].unsqueeze(1).broadcast_to([P, NTAP, P]),
                                   w.unsqueeze(2).broadcast_to([P, NTAP, P]), ALU.mult).then_inc(s_dg, 1)

            def ad(b, s, j, *_):
                pool.wait_ge(s_sp1, done(b, 4, s))
                pool.tensor_tensor(dtb[:, s % 2, j, :], dtb[:, s % 2, j, :], dub[:, s % 2, j, :], ALU.add)\
                    .then_inc(s_ad, 1)

            def dm(b, s, j, *_):
                pool.wait_ge(s_ad, done(b, 16, 4 * s + j))
                pool.tensor_tensor(dub[:, s % 2, j, :], dtb[:, s % 2, j, :], us[:, j, :], ALU.mult).then_inc(s_dm, 1)

            def yo(b, s, k, *_):
                back = s // 2
                pool.wait_ge(tk_["yo"], done(b, 16, 4 * s + k))
                pool.wait_ge(s_hyl[k % 2], 16 * done(b, 8, 2 * s + k // 2))
                dst = x2f[:, tile_of(s, k), :] if back else hyt[:, k % 2, :]
                pool.tensor_tensor(dst, hyt[:, k % 2, :], ytmp[:], ALU.add).then_inc(s_yadd, 1)

            def l_h(b, s, i, *_):
                pool.wait_ge(s_ln, done(b, 2, i // 2))
                pool.wait_ge(s_modl, 16 * (b + 1))
                modulate(b, i, modl, s_lh1, s_lh)

            def l_rn(b, *_):
                pool.wait_ge(s_sq, done(b, 1, 0))
                pool.tensor_tensor(rsx[:, 3, :], ve[:, 3, :], mhalf[:, 0:NT], ALU.pow).then_inc(s_rn1, 1)
                wait_apart(pool, (s_rn1, done(b, 1, 0)))
                pool.tensor_scalar(rsx[:, 3, :], rsx[:, 3, :], 1e12, None, ALU.min).then_inc(s_rn, 1)

            def M(b, s, i, *_):
                pool.wait_ge(tk_["PV"], done(b, 8, i))
                if i:
                    pool.wait_ge(pe_["OT"], done(b, 8, i - 1))
                w = rw[:, i, :].rearrange("p (k e) -> p k e", k=NT)
                pool.tensor_tensor(mixed.rearrange("p k (e d) -> p k e d", e=2),
                                   attn[:].unsqueeze(1).unsqueeze(1).broadcast_to([P, NT, 2, HD]),
                                   w.unsqueeze(3).broadcast_to([P, NT, 2, HD]), ALU.mult).then_inc(s_mix, 1)

            def FO(b, s, i, *_):
                pool.wait_ge(tk_["FO"], done(b, 8, i))
                pool.tensor_tensor(ft[:, i % 2, :], ft[:, i % 2, :], x2f[:, i, :], ALU.add).then_inc(s_fadd, 1)

            def core(b, s, n, seg):
                if seg == "prologue":
                    return
                i = NS * s + n
                if n == 0:
                    pool.wait_ge(s_dm, done(b, 16, 4 * s + 3))
                pool.wait_ge(s_bc, done(b, STEPS, i))
                for j in range(J):
                    r = 4 * i + j
                    need(pool, s_scan, done(b, 4 * STEPS, r - RING))
                    pool.tensor_tensor(binp[:, r % RING, :], dub[:, s % 2, j, :], bbc[:, i % 2, :], ALU.mult)\
                        .then_inc(s_in, 1)

            walk(pool, {"p_pw": p_pw, "p_pw2": p_pw2, "l_pw": l_pw, "p_h": p_h, "p_base": p_base, "dg": dg, "ad": ad,
                        "dm": dm, "yo": yo, "l_h": l_h, "l_rn": l_rn, "M": M, "FO": FO}, core, lambda: None)

        @block.vector
        def _(dve):
            dve.wait_ge(s_pec, 1)
            dve.tensor_copy(simrn, hT[3][:, 0:NE]).then_inc(s_vc, 1)
            m6 = mods.rearrange("p m c -> p (m c)")
            for m in range(3):
                dve.tensor_copy(m6[:, 512 * m:512 * (m + 1)], hT[m][0:B, :])
            dve.tensor_scalar(gsgn[0], hT[1][0:B, 0:D], 0.0, 2.0, ALU.is_ge, ALU.mult)
            dve.tensor_scalar(gsgn[1], hT[2][0:B, D:2 * D], 0.0, 2.0, ALU.is_ge, ALU.mult).then_inc(s_vc, 1)
            dve.wait_ge(s_vc, 2)
            for q in range(2):
                ins = dve.tensor_scalar(gsgn[q], gsgn[q], -1.0, None, ALU.add)
            ins.then_inc(s_vc, 1)
            dve.wait_ge(s_vc, 3)
            for q, m in enumerate((2, 5)):
                ins = dve.tensor_tensor(mods[:, m, :], mods[:, m, :], gsgn[q], ALU.mult)
            ins.then_inc(s_vc, 1)
            dve.wait_ge(s_vc, 4)
            for q, m in enumerate((2, 5)):
                ins = dve.tensor_scalar(mods[:, m, :], mods[:, m, :], 0.25, None, ALU.max)
            ins.then_inc(s_vc, 1)
            dve.wait_ge(s_vc, 5)
            for q, m in enumerate((2, 5)):
                ins = dve.tensor_tensor(mods[:, m, :], mods[:, m, :], gsgn[q], ALU.mult)
            ins.then_inc(s_vc, 1)
            for m in (1, 4):
                ins = dve.tensor_scalar(mods[:, m, :], mods[:, m, :], 1.0, None, ALU.add)
            ins.then_inc(s_vc, 1)
            dve.wait_ge(s_vc, 7)
            dve.engine_nop().then_inc(s_mods, 1)
            dve.wait_ge(s_pc, 6)
            dve.engine_nop().then_inc(s_vc, 1)
            dve.wait_ge(s_modst, 16)
            dve.engine_nop().then_inc(s_vc, 1)

            def stats(src, mv, b, s_st, s_ag, parts=1, i=0):
                tiles = range(NT // parts * i, NT // parts * (i + 1))
                for t in tiles:
                    ins = dve.bn_stats(stx[:, t, :], src[:, t, :])
                ins.then_inc(s_st, 1)
                wait_apart(dve, (s_st, done(b, parts, i)))
                for t in tiles:
                    ins = dve.bn_aggr(mv[:, t, :], stx[:, t, :])
                ins.then_inc(s_ag, 1)

            def normalise(dst, src, mv, w, i, s_end):
                for t in range(4 * i, 4 * i + 4):
                    ins = dve.tensor_scalar(dst[:, t, :], src[:, t, :], mv[:, t, 0:1], rsx[:, w, t:t + 1],
                                            ALU.subtract, ALU.mult)
                ins.then_inc(s_end, 1)

            def p_st(b, *_):
                dve.wait_ge(s_x, 16 * (b + 1))
                stats(bufx, mvx, b, s_stx, s_aggx)

            def p_n(b, s, i, *_):
                dve.wait_ge(s_pw, done(b, 1, 0))
                need(dve, s_pb, done(b - 1, 4, 3))
                normalise(bufh, bufx, mvx, 0, i, s_pn)

            def p_st2(b, s, i, *_):
                dve.wait_ge(s_ph, done(b, 4, 2 * i + 1))
                stats(bufh, mvh, b, s_sth, s_aggh, 2, i)

            def p_xn(b, s, i, *_):
                dve.wait_ge(s_pw2, done(b, 2, i))
                normalise(xnt, bufh, mvh, 1, i, s_pxn)

            def Xr(b, s, *_):
                hi, _mid, rest = b_split(s)
                dve.wait_ge(tk_["X"], done(b, 4, s))
                dve.scalar_tensor_tensor(rest, hi, part[:, 0:1], xd[:], ALU.mult, ALU.add).then_inc(s_brest, 1)

            def Xl(b, s, *_):
                _hi, mid, rest = b_split(s)
                dve.wait_ge(s_bmid, done(b, 4, s))
                dve.scalar_tensor_tensor(bparts[:, s % 2, :], mid, part[:, 1:2], rest, ALU.mult, ALU.add)\
                   .then_inc(s_bparts, 1)

            def yT(b, s, k, bk, *_):
                back, half, lo = unit(s)
                at = (tile_of(s, k) - lo // P) * P
                dve.wait_ge(pe_["yT"], done(b, 16, 4 * s + k))
                dve.wait_ge(s_zs, done(b, 4, s))
                need(dve, pe_["yo"], done(b, 16, 4 * s + k - 2))
                y = bk[0][:].rearrange("p (j t) -> p j t", j=J)
                dve.tensor_tensor(yg[:, k % 2], y[:, :, ::-1] if back else y, sz[:, :, at:at + P], ALU.mult)\
                   .then_inc(tk_["yT"], 1)

            def yo(b, s, k, bk, *_):
                dve.wait_ge(pe_["yo"], done(b, 16, 4 * s + k))
                need(dve, s_yadd, done(b, 16, 4 * s + k - 1))
                dve.wait_ge(s_ga, 16 * (b + 1))
                dve.tensor_tensor(ytmp[:], bk[0][:, 0:D], ga_bc[:], ALU.mult).then_inc(tk_["yo"], 1)

            def l_st(b, *_):
                dve.wait_ge(s_yadd, done(b, 16, 15))
                stats(x2f, mvl, b, s_stl, s_aggl)

            def l_n(b, s, i, bk, tn, seg):
                dve.wait_ge(s_pw3, done(b, 1, 0))
                dve.wait_ge(s_pb, 4 * B if seg == "epilogue" else done(b + 1, 4, 3))
                normalise(bufh, x2f, mvl, 2, i, s_ln)

            def l_lg(b, s, _k, bk, tn, seg):
                at = [0]

                def step(ins):
                    ins.then_inc(s_gate, 1)
                    dve.wait_ge(s_gate, done(b, NGATE, at[0]))
                    at[0] += 1

                def over(v):
                    return v.unsqueeze(2).broadcast_to([P, NT, NE])

                def experts(v):
                    return v.unsqueeze(1).broadcast_to([P, NT, NE])

                G, LG, ON, K, S1, S2 = gt
                m0, m1, m2 = small[:, 0, :], small[:, 1, :], small[:, 2, :]
                dve.wait_ge(pe_["l_lg"], done(b, 1, 0))
                dve.wait_ge(s_rn, done(b, 1, 0))
                dve.wait_ge(s_base, 16 * B if seg == "epilogue" else 16 * (b + 2))
                step(dve.tensor_tensor(LG, bk[0][:, 0:NT * NE].rearrange("p (t e) -> p t e", t=NT),
                                       over(rsx[:, 3, :]), ALU.mult))
                step(dve.tensor_tensor(LG, LG, experts(sgate[:]), ALU.subtract))
                step(dve.tensor_scalar(G, LG, 0.0, None, ALU.max))
                step(dve.tensor_scalar(ON, G, 0.0, None, ALU.is_gt))
                step(dve.tensor_reduce(m0, ON, AX, ALU.max))
                step(dve.tensor_scalar(m0, m0, -1.0, 1.0, ALU.mult, ALU.add))
                for src, pick in ((LG, S1), (S2, S2)):
                    step(dve.tensor_reduce(m1, src, AX, ALU.max))
                    step(dve.tensor_tensor(K, src, over(m1), ALU.is_equal))
                    step(dve.tensor_tensor(K, K, experts(rank[:]), ALU.mult))
                    step(dve.tensor_reduce(m2, K, AX, ALU.max))
                    step(dve.tensor_tensor(pick, K, over(m2), ALU.is_equal))
                    if pick is S1:
                        step(dve.scalar_tensor_tensor(S2, S1, -BIG, LG, ALU.mult, ALU.add))
                step(dve.tensor_tensor(S1, S1, S2, ALU.add))
                step(dve.tensor_tensor(S1, S1, over(m0), ALU.mult))
                step(dve.tensor_tensor(ON, ON, S1, ALU.max))
                step(dve.tensor_reduce(m1, G, AX, ALU.max))
                step(dve.tensor_tensor(G, G, over(m1), ALU.subtract))
                assert at[0] == NGATE, at

            def l_gt(b, s, _k, bk, tn, seg):
                G, ON, m1, m2 = gt[0], gt[2], small[:, 1, :], small[:, 2, :]
                dve.wait_ge(s_gexp, done(b, 1, 0))
                dve.tensor_tensor(G, G, ON, ALU.mult).then_inc(s_gate2, 1)
                dve.wait_ge(s_gate2, done(b, 4, 0))
                dve.tensor_reduce(m1, G, AX, ALU.add).then_inc(s_gate2, 1)
                dve.wait_ge(s_gate2, done(b, 4, 1))
                dve.reciprocal(m2, m1).then_inc(s_gate2, 1)
                dve.wait_ge(s_gate2, done(b, 4, 2))
                dve.tensor_tensor(rw[:], G, m2.unsqueeze(2).broadcast_to([P, NT, NE]), ALU.mult).then_inc(s_gate2, 1)
                dve.wait_ge(s_gate2, done(b, 4, 3))

            def q(b, s, i, bk, *_):
                g, pair = i // 4, i % 4
                dve.wait_ge(pe_["q"], done(b, 32, i))
                if i == 0:
                    dve.wait_ge(pe_["l_T"], done(b, 4, 3))
                    dve.wait_ge(s_sq, done(b, 1, 0))
                for e in range(EC):
                    for h in range(2):
                        t, ex = 2 * pair + h, EC * g + e
                        v, src, w = qkvb[:, t, :], bk[h][:, e * QW:(e + 1) * QW], rw[:, t, ex:ex + 1]
                        if ex == 0:
                            ins = dve.tensor_scalar(v, src, w, None, ALU.mult)
                        else:
                            dve.wait_ge(s_qst, done(b, 128, 4 * i + 2 * e + h - 2 if e else 4 * (i - 4) + 2 + h))
                            ins = dve.scalar_tensor_tensor(v, src, w, v, ALU.mult, ALU.add)
                        ins.then_inc(s_qst, 1)

            def S(b, s, i, bk, tn, seg):
                dve.wait_ge(pe_["S"], done(b, 8, i))
                if i:
                    dve.wait_ge(pe_["PT"], done(b, 8, i - 1))
                if i == 0:
                    dve.wait_ge(s_gate2, done(b, 4, 3))
                for h in range(len(bk)):
                    w = min(i * P - 512 * h, 512)
                    if w > 0:
                        dve.tensor_copy(prob[:, 512 * h:512 * h + w], bk[h][:, 0:w])
                o = (i * P) % 512
                dve.tensor_tensor(prob[:, i * P:(i + 1) * P], bk[-1][:, o:o + P], causal[:], ALU.add).then_inc(s_s, 1)
                dve.wait_ge(s_s, done(b, 16, 2 * i))
                dve.tensor_reduce(mxs[:, 2:3], prob[:, 0:(i + 1) * P], AX, ALU.max).then_inc(s_s, 1)
                dve.wait_ge(s_s, done(b, 16, 2 * i + 1))
                if i:
                    dve.wait_ge(s_exp, done(b, 8, i - 1))
                dve.tensor_scalar(mxs[:, 3:4], mxs[:, 2:3], -(HD ** -0.5), None, ALU.mult).then_inc(tk_["S"], 1)

            def PV(b, s, i, bk, tn, seg):
                dve.wait_ge(s_exp, done(b, 8, i))
                dve.reciprocal(rsum[:, 1:2], rsum[:, 0:1]).then_inc(s_ri, 1)
                dve.wait_ge(s_ri, done(b, 8, i))
                dve.wait_ge(pe_["PV"], done(b, 8, i))
                if i:
                    dve.wait_ge(s_mix, done(b, 8, i - 1))
                dve.tensor_scalar(attn[:], bk[0][:, 0:HD], rsum[:, 1:2], None, ALU.mult).then_inc(tk_["PV"], 1)

            def FO(b, s, i, bk, tn, seg):
                dve.wait_ge(pe_["FO"], done(b, 8, i))
                if i < 2:
                    dve.wait_ge(s_pb, 4 * B if seg == "epilogue" else done(b + 1, 4, 3))
                if i >= 2 or seg == "epilogue":
                    dve.wait_ge(s_out[i % 2], 16 * done(b, 4, i // 2 - 1))
                dve.wait_ge(s_gb, 16 * (b + 1))
                dve.tensor_tensor(ft[:, i % 2, :], bk[0][:, 0:D], gb_bc[:], ALU.mult).then_inc(tk_["FO"], 1)

            def read_out(b, i, t):
                s, n = i // NS if i >= 0 else NU - 1, i % NS
                dve.wait_ge(s_turn, done(b, 4 * STEPS, 4 * i + t))
                if n == 0:
                    dve.wait_ge(tk_["W"], done(b, 16, 4 * (i // NS) + 3))
                    dve.wait_ge(tk_["C"], done(b, 4, i // NS))
                need(dve, s_acc, done(b, 4 * STEPS, 4 * (i - 1) + t))
                dve.scalar_tensor_tensor(acc[:, s % 2, t, :], hT[t][:], ct[:, s % 2, t, n:n + 1],
                                         acc[:, s % 2, t, :], ALU.mult, ALU.add).then_inc(s_acc, 1)

            def core(b, s, n, seg):
                if seg == "prologue":
                    return
                i, half = NS * s + n, s % 2
                for j in range(J):
                    r = 4 * i + j
                    dve.wait_ge(s_dec, done(b, 4 * STEPS, r))
                    dve.wait_ge(s_in, done(b, 4 * STEPS, r))
                    if j == 0:
                        need(dve, s_turn, done(b, 4 * STEPS, 4 * (i - 2) + 3))
                        if half:
                            dve.wait_ge(s_car, done(b, 2 * NS, NS * (s // 2) + n))
                    first = carry[:, j, n:n + 1] if half else 0.0
                    dve.tensor_tensor_scan(hst[:, i % 2, j, :], decay[:, r % RING, :], binp[:, r % RING, :], first,
                                           ALU.mult, ALU.add).then_inc(s_scan, 1)
                    if not (seg == "first" and i == 0):
                        read_out(b, i - 1, j)
                if not half:
                    dve.wait_ge(s_scan, done(b, 4 * STEPS, 4 * i + 3))
                    dve.tensor_copy(carry[:, :, n], hst[:, i % 2, :, UL - 1]).then_inc(s_car, 1)

            walk(dve, {"p_st": p_st, "p_n": p_n, "p_st2": p_st2, "p_xn": p_xn, "Xr": Xr, "Xl": Xl, "yT": yT, "yo": yo,
                       "l_st": l_st,
                       "l_n": l_n, "l_lg": l_lg, "l_gt": l_gt, "q": q, "S": S, "PV": PV, "FO": FO},
                 core, lambda: [read_out(B - 1, STEPS - 1, t) for t in range(UT)])


def kernel(**inputs):
    import numpy as np
    import concourse.bacc as bacc
    from concourse.bass_utils import run_bass_kernel_spmd

    g = {k: np.asarray(v) for k, v in inputs.items()}

    def blocks(w):
        return w.reshape(-1, P, w.shape[-1]).transpose(1, 0, 2)

    arr = {"x": g["L0_attn_x"]}
    for d in "fb":
        q = lambda name: g[f"L0_attn_{d}_{name}"]
        arr[f"win_{d}"] = blocks(q("Win").T)
        arr[f"wx_{d}"] = blocks(q("Wx").T)
        arr[f"wdt_{d}"] = q("Wdt").T
        arr[f"wout_{d}"] = blocks(q("Wout").T)
        arr[f"convw_{d}"] = blocks(q("convw").reshape(DI, NTAP))
        arr[f"vecs_{d}"] = np.stack([q("convb"), q("bdt"), q("D")]).reshape(3, J, P).transpose(2, 0, 1)
        arr[f"alog_{d}"] = blocks(q("Alog"))
    arr["norm"] = np.stack([g["L0_attn_norm_g"], g["L0_attn_norm_b"]]).reshape(2, KD, P).transpose(2, 0, 1)
    w = np.stack([g["L0_ffn_q_proj"], g["L0_ffn_k_proj"], g["L0_ffn_v_proj"]])
    arr["wqkv"] = w.reshape(3, NCH, EC, KD, P, HD).transpose(1, 4, 3, 2, 0, 5).reshape(NCH, P, KD, EC * QW)
    arr["wo"] = blocks(g["L0_ffn_o_proj"].reshape(NE * HD, D))
    arr["sim"] = blocks(g["L0_ffn_sim_matrix"])
    arr["gates"] = g["L0_ffn_gates"]
    arr["rank"] = np.arange(NE, 0, -1, dtype=np.float32)
    arr["cT"] = blocks(g["L0_c"].T)
    arr["wmod"] = blocks(g["L0_wmod"])
    arr = {k: np.ascontiguousarray(v) for k, v in arr.items()}

    nc = bacc.Bacc("TRN2", target_bir_lowering=False, num_devices=1)
    aps = {k: nc.dram_tensor(f"in_{k}", v.shape, F32, kind="ExternalInput").ap() for k, v in arr.items()}
    out = nc.dram_tensor("out", (B, L, D), F32, kind="ExternalOutput").ap()
    mod_d = nc.dram_tensor("mod_scratch", (B, 6, D), F32).ap()
    hy_d = nc.dram_tensor("partial_scratch", (B, L, D), F32).ap()
    program(nc, aps, out, mod_d, hy_d)
    r = run_bass_kernel_spmd(nc, [{f"in_{k}": v for k, v in arr.items()}], core_ids=[0])
    return r.results[0]["out"]
```
